# Optimizing a Trainium2 kernel written in Bass

```python
import numpy as np
import jax
import jax.numpy as jnp

def _softmax(x, axis=-1):
    return jax.nn.softmax(x, axis=axis)

def _gelu(x):
    return jax.nn.gelu(x, approximate=True)

def _silu(x):
    return jax.nn.silu(x)

def _sigmoid(x):
    return jax.nn.sigmoid(x)

def _layernorm(x, axis=-1, eps=1e-05):
    m = jnp.mean(x, axis=axis, keepdims=True)
    v = jnp.var(x, axis=axis, keepdims=True)
    return (x - m) / jnp.sqrt(v + eps)

def _scatter_add(tgt, idx, src, axis=0):
    return tgt.at[idx].add(src)

def _segment_sum(src, seg, n):
    return jax.ops.segment_sum(src, seg, n)
kernel_name = 'mk_gnn_resnorm_d2_gnn_r8_f7e8a9'

def setup_inputs(seed: int=0):
    np.random.seed(seed)
    _w = jnp.asarray

    def _rec_inputs():
        import jax
        import jax.numpy as jnp
        _gk = jax.random.key(seed)
        x = -0.0002117 + 1 * jax.random.normal(jax.random.fold_in(_gk, 1), (6250, 512), jnp.float32)
        src = jax.random.randint(jax.random.fold_in(_gk, 2), (100000,), 0, 6250, jnp.int32)
        dst = jnp.minimum((6250 * jax.random.uniform(jax.random.fold_in(_gk, 3), (100000,)) ** 2.0).astype(jnp.int32), 49999)
        _o = jnp.argsort(dst, stable=True)
        src = src[_o]
        dst = dst[_o]
        edge_weight = jax.random.uniform(jax.random.fold_in(_gk, 12), (100000,), jnp.float32, 0.0, 1)
        return (x, src, dst, edge_weight)
    x, src, dst, edge_weight = _rec_inputs()

    def _L0_gnn_setup():
        import jax, jax.numpy as jnp
        import numpy as np
        N_NODES = 6250
        N_EDGES = 200000
        D_IN = 512
        D_OUT = 512
        key = jax.random.key(seed)
        k_x, k_w, k_b, k_r, k_c, k_e = jax.random.split(key, 6)
        x = jax.random.normal(k_x, (N_NODES, D_IN), dtype=jnp.float32)
        stdv = 1.0 / np.sqrt(D_OUT)
        weight = jax.random.uniform(k_w, (D_IN, D_OUT), minval=-stdv, maxval=stdv, dtype=jnp.float32)
        bias = jax.random.uniform(k_b, (D_OUT,), minval=-stdv, maxval=stdv, dtype=jnp.float32)
        row = jax.random.randint(k_r, (N_EDGES,), 0, N_NODES, dtype=jnp.int32)
        col = jax.random.randint(k_c, (N_EDGES,), 0, N_NODES, dtype=jnp.int32)
        edge_weight = jax.random.uniform(k_e, (N_EDGES,), dtype=jnp.float32)
        return {'x': x, 'weight': weight, 'bias': bias, 'row': row, 'col': col, 'edge_weight': edge_weight}
    _L0_gnn_all = _L0_gnn_setup()
    _L0_gnn_in = {k: v for k, v in _L0_gnn_all.items() if k in ('weight', 'bias')}
    del _L0_gnn_all

    def _L1_gnn_setup():
        import jax, jax.numpy as jnp
        import numpy as np
        N_NODES = 6250
        N_EDGES = 100000
        D_IN = 512
        D_OUT = 512
        key = jax.random.key(seed)
        k1, k2, k3, k4, k5 = jax.random.split(key, 5)
        local_feats = jax.random.normal(k1, (N_NODES, D_IN), dtype=jnp.float32)
        src = jax.random.randint(k2, (N_EDGES,), 0, N_NODES, dtype=jnp.int64)
        dst = jax.random.randint(k3, (N_EDGES,), 0, N_NODES, dtype=jnp.int64)
        lim = (6.0 / (D_IN + D_OUT)) ** 0.5
        W_self = jax.random.uniform(k4, (D_OUT, D_IN), minval=-lim, maxval=lim, dtype=jnp.float32)
        W_neigh = jax.random.uniform(k5, (D_OUT, D_IN), minval=-lim, maxval=lim, dtype=jnp.float32)
        b = jnp.zeros((D_OUT,), dtype=jnp.float32)
        return {'local_feats': local_feats, 'src': src, 'dst': dst, 'layer': 0, 'W_self': W_self, 'W_neigh': W_neigh, 'b': b}
    _L1_gnn_all = _L1_gnn_setup()
    _L1_gnn_in = {k: v for k, v in _L1_gnn_all.items() if k in ('W_self', 'W_neigh', 'b')}
    del _L1_gnn_all
    return {'x': x, 'src': src, 'dst': dst, 'edge_weight': edge_weight, 'L0_gnn_weight': _L0_gnn_in['weight'], 'L0_gnn_bias': _L0_gnn_in['bias'], 'L1_gnn_W_self': _L1_gnn_in['W_self'], 'L1_gnn_W_neigh': _L1_gnn_in['W_neigh'], 'L1_gnn_b': _L1_gnn_in['b']}

def reference(x, src, dst, edge_weight, L0_gnn_weight, L0_gnn_bias, L1_gnn_W_self, L1_gnn_W_neigh, L1_gnn_b):
    import jax
    import jax.numpy as jnp

    def _L0_gnn_ref(x, weight, bias, row, col, edge_weight):
        import jax, jax.numpy as jnp
        import numpy as np
        N_NODES = 6250
        N_EDGES = 200000
        D_IN = 512
        D_OUT = 512
        support = x @ weight
        msgs = edge_weight[:, None] * support[col]
        out = jax.ops.segment_sum(msgs, row, num_segments=N_NODES)
        return out + bias

    def _L1_gnn_ref(local_feats, src, dst, layer, W_self, W_neigh, b):
        import jax, jax.numpy as jnp
        import numpy as np
        N_NODES = 6250
        N_EDGES = 100000
        D_IN = 512
        D_OUT = 512
        'DistSAGEConv forward: mean neighbor aggregation + fc_self + fc_neigh + bias + ReLU.\n            `layer` only selects which hop in the distributed impl; aggregation math is identical.\n            '
        n = local_feats.shape[0]
        msg = local_feats[src]
        agg = jax.ops.segment_sum(msg, dst, num_segments=n)
        deg = jax.ops.segment_sum(jnp.ones((src.shape[0],), local_feats.dtype), dst, num_segments=n)
        h_neigh = agg / jnp.maximum(deg, 1.0)[:, None]
        rst = local_feats @ W_self.T + h_neigh @ W_neigh.T + b
        return jax.nn.relu(rst)
    x = _layernorm(x + _L0_gnn_ref(x, L0_gnn_weight, L0_gnn_bias, src, dst, edge_weight), axis=-1)
    x = _layernorm(x + _L1_gnn_ref(x, src, dst, 0, L1_gnn_W_self, L1_gnn_W_neigh, L1_gnn_b), axis=-1)
    return x

_drawn_inputs = setup_inputs


def setup_inputs(seed=0):
    import zlib

    import numpy as np

    out = dict(_drawn_inputs(seed))
    spreads = {'L1_gnn_b': (0.0, 0.1)}
    factors = {'L0_gnn_bias': 3.098}
    for name, (base, spread) in spreads.items():
        noise = np.random.default_rng([zlib.crc32(name.encode()), seed]).standard_normal(out[name].shape)
        drawn = base * np.exp(spread * noise) if base else spread * noise
        out[name] = jnp.asarray(drawn.astype(out[name].dtype))
    for name, factor in factors.items():
        out[name] = (out[name] * factor).astype(out[name].dtype)
    return out
```

```python
from contextlib import ExitStack

import concourse.bass as bass
from concourse import mybir

F32 = mybir.dt.float32
F32R = mybir.dt.float32r
I32 = mybir.dt.int32
U32 = mybir.dt.uint32
ALU = mybir.AluOpType
ACT = mybir.ActivationFunctionType
AX = mybir.AxisListType

P = 128
CHUNK = 128
GROUP = 4
RING = 4
SEL = 2
MSG = 2 * GROUP
ACCS = GROUP
LEAD = 2
EPS = 1e-5
NO_ROW = 1000.0
FAR = 8192.0


def gnn_two_layers(nc, x, src_t, dst_t, w_t, src_n, dst_n, w0, b0, w_self, w_neigh, b1, out):
    rows, D = x.shape
    BLOCKS = rows // P
    CHUNKS = src_t.shape[1]
    GROUPS = CHUNKS // GROUP
    ROUNDS = GROUPS // RING
    HALF = GROUPS // 2
    KT = D // P
    GE = GROUP * CHUNK
    assert BLOCKS % 2 == 1 and BLOCKS >= 5 and GROUPS % RING == 0 and ROUNDS >= 3

    x1_dram = nc.dram_tensor("x1_dram", [rows, D], F32).ap()
    acc_tensors = [nc.dram_tensor(f"acc{k}", [rows + P, D], F32).ap() for k in range(ACCS)]
    base_dram = nc.dram_tensor("base_dram", [GROUPS], I32).ap()
    wide_dram = nc.dram_tensor("wide_dram", [GROUPS], I32).ap()

    ctx = ExitStack()
    with ctx:
        def sb(name, shape, dt=F32):
            return ctx.enter_context(nc.sbuf_tensor(name, shape, dt))

        def ps(name):
            return ctx.enter_context(nc.psum_tensor(name, [P, 512], F32))

        def sem(name):
            return ctx.enter_context(nc.semaphore(name))

        def lender(flat):
            taken = [0]

            def lend(*shape, parts=P):
                n = 1
                for k in shape:
                    n *= k
                a = flat[0:parts, taken[0]:taken[0] + n]
                taken[0] += n
                assert taken[0] <= flat.shape[1]
                if len(shape) == 2:
                    a = a.rearrange("p (a b) -> p a b", a=shape[0])
                if len(shape) == 3:
                    a = a.rearrange("p (a b c) -> p a b c", a=shape[0], b=shape[1])
                return a

            return lend, taken

        agg = sb("agg", [P, BLOCKS + 1, D])
        deg = sb("deg", [P, BLOCKS + 1])
        gathered = sb("gathered", [P, RING * GROUP, D])
        sel = sb("sel", [P, SEL, GROUP, P], F32R)
        idx_all = sb("idx_all", [P, CHUNKS], I32)
        idx_now = [sb(f"idx_now{g}", [P, GROUP], I32) for g in range(RING)]
        to_now = [sb(f"to_now{g}", [P, GROUP], I32) for g in range(RING)]
        dst_f = sb("dst_f", [P, CHUNKS])
        row_f = sb("row_f", [P, CHUNKS])
        in_lo = sb("in_lo", [P, GROUPS])
        in_hi = sb("in_hi", [P, GROUPS])
        blk_i = sb("blk_i", [1, GROUPS], I32)
        any_f = sb("any_f", [1, 1])
        any_wide = sb("any_wide", [1, 1], I32)
        g_max = sb("g_max", [HALF, 2])
        g_min = sb("g_min", [HALF, 2])
        g_base = sb("g_base", [HALF, 2], I32)
        g_wide_f = sb("g_wide_f", [HALF, 2])
        g_wide = sb("g_wide", [HALF, 2], I32)
        col_f = sb("col_f", [P, P])
        par_i = sb("par_i", [P, 1], I32)
        par_f = sb("par_f", [P, 1])
        ident = sb("ident", [P, P])
        tri = sb("tri", [P, P])
        ones = sb("ones", [P, P])
        ones_r = sb("ones_r", [P, 2], F32R)
        zeros = sb("zeros", [P, D])
        eps = sb("eps", [P, 1])
        w_a = sb("w_a", [P, KT, D])
        w_s = sb("w_s", [P, KT, D])
        bias = [sb(f"bias{l}", [1, D]) for l in range(2)]
        far_dst = sb("far_dst", [P, GROUP])
        staged = sb("staged", [P, 2, D])
        xin = sb("xin", [P, 2, D])
        agg_t = sb("agg_t", [P, 2, KT, P])
        x_t = sb("x_t", [P, 2, KT, P])
        y = sb("y", [P, 2, D])
        xo = sb("xo", [P, 2, D])
        stats = sb("stats", [P, 2, 6])
        mv = sb("mv", [P, 2, 2])
        std = sb("std", [P, 2, 1])
        rstd = sb("rstd", [P, 2, 1])
        shift = sb("shift", [P, 2, 1])
        deg1 = sb("deg1", [P, 2, 1])
        rdeg = sb("rdeg", [P, 2, 1])

        lend, _ = lender(gathered[:].rearrange("p a d -> p (a d)"))
        dn_i = lend(2, GE, parts=HALF).bitcast(I32)
        dn_f = lend(2, GE, parts=HALF)
        dn_pad = lend(2, GE, parts=HALF)
        dst_i = lend(CHUNKS).bitcast(I32)
        row_i = lend(CHUNKS).bitcast(I32)
        pad_f = lend(CHUNKS)
        gat_f = lend(CHUNKS)
        base_i = lend(GROUPS).bitcast(I32)
        brow_i = lend(GROUPS).bitcast(I32)
        brow_f = lend(GROUPS)
        wide_row = lend(GROUPS, parts=1).bitcast(I32)
        wide_f = lend(GROUPS, parts=1)
        col_i = lend(P).bitcast(I32)

        lend, lent = lender(agg[:].rearrange("p a d -> p (a d)"))
        msg = lend(MSG, D)
        same = lend(SEL, GROUP, P)
        src_all = lend(SEL, GE).bitcast(I32)
        accs = lend(2, ACCS * D)
        scratch = lend(GROUP, P)
        src_f = lend(CHUNKS)
        spare_f = lend(CHUNKS)
        gat_all = lend(CHUNKS).bitcast(I32)
        wgt = lend(CHUNKS)
        earlier = lend(SEL, GROUP)
        to_f = lend(SEL, GROUP)
        spare_row = lend(1)
        lent_blocks = -(-lent[0] // D)

        banks = [ps(f"bank{k}") for k in range(7)]
        psum_msg = banks[0:GROUP]
        psum_sum = banks[0:SEL]
        psum_deg = banks[SEL:2 * SEL]
        psum_t, psum_xt, psum_y = banks[4:7]

        edges_in = sem("edges_in")
        dstn_in = sem("dstn_in")
        w_in = sem("w_in")
        wn_in = sem("wn_in")
        base_out = sem("base_out")
        base_in = sem("base_in")
        iotas = sem("iotas")
        prep = sem("prep")
        zeros_ready = sem("zeros_ready")
        acc_zero = sem("acc_zero")
        flag_ready = sem("flag_ready")
        agg_zero = sem("agg_zero")
        waited = sem("waited")
        layer_summed = sem("layer_summed")

        idx0_ready = sem("idx0_ready")
        rows0_in = [sem(f"rows0_in{k}") for k in range(RING * GROUP)]
        src_all_in = [sem(f"src_all_in{q}") for q in range(SEL)]
        same_ready = sem("same_ready")
        counted = sem("counted")
        aimed = sem("aimed")
        to_ready = sem("to_ready")
        msg_summed = sem("msg_summed")
        msg_ready = sem("msg_ready")
        msg_added = [sem(f"msg_added{m}") for m in range(MSG)]
        idx_ready = sem("idx_ready")
        rows_in = [sem(f"rows_in{k}") for k in range(RING * GROUP)]
        sel_ready = sem("sel_ready")
        summed = sem("summed")
        added = sem("added")

        class Dense:
            def __init__(self, l):
                self.xin_ready = [sem(f"xin_ready{l}{q}") for q in range(2)]
                self.staged = sem(f"staged{l}")
                self.transposed = sem(f"transposed{l}")
                self.t_ready = sem(f"t_ready{l}")
                self.projected = sem(f"projected{l}")
                self.y_ready = sem(f"y_ready{l}")
                self.stat = sem(f"stat{l}")
                self.var_ready = sem(f"var_ready{l}")
                self.std_ready = sem(f"std_ready{l}")
                self.rstd_ready = sem(f"rstd_ready{l}")
                self.norm_ready = sem(f"norm_ready{l}")
                self.normed = sem(f"normed{l}")
                self.stored = [sem(f"stored{l}{q}") for q in range(2)]

        dense = [Dense(l) for l in range(2)]
        accs_in = [sem(f"accs_in{q}") for q in range(2)]
        acc_sum = sem("acc_sum")
        deg1_ready = sem("deg1_ready")
        rdeg_ready = sem("rdeg_ready")

        def row_of(t, b):
            return t[:, b, :] if isinstance(b, int) else t[:, bass.ds(b, 1), :].rearrange("p o d -> p (o d)")

        def general(eng):
            return eng.value_load(any_wide[0:1, 0:1], min_val=0, max_val=1)

        def alone(eng):
            eng.sem_inc(waited, 1)

        def rounds(eng, one_round):
            one_round(0, True, False)
            with eng.Fori(1, ROUNDS - 1) as r:
                one_round(r, False, False)
            one_round(ROUNDS - 1, False, True)

        def block_steps(eng, step):
            step(0, 0, True, 2)
            step(1, 1, True, 2)
            step(2, 0, False, 2)
            with eng.Fori(3, BLOCKS - 3, 2) as i:
                step(i, 1, False, 2)
                step(i + 1, 0, False, 2)
            step(BLOCKS - 2, 1, False, 1)
            step(BLOCKS - 1, 0, False, 0)

        def half(i, q):
            return (i - q) // 2

        def all_stored(eng, d):
            eng.wait_ge(d.stored[0], 16 * (BLOCKS // 2 + 1))
            eng.wait_ge(d.stored[1], 16 * (BLOCKS // 2))

        block = ctx.enter_context(nc.Block())

        @block.sync
        def _(sp):
            sp.dma_start(dn_i, dst_n.rearrange("(p t) e -> p t e", p=HALF)).then_inc(dstn_in, 16)
            for t, a in ((idx_all[:], src_t), (dst_i, dst_t), (wgt, w_t)):
                sp.dma_start(t, a).then_inc(edges_in, 16)
            sp.wait_ge(zeros_ready, 1)
            for k in range(ACCS):
                sp.dma_start(acc_tensors[k].rearrange("(b p) d -> p b d", p=P),
                             zeros[:].rearrange("p (o d) -> p o d", o=1).broadcast_to([P, BLOCKS + 1, D])).then_inc(acc_zero, 16)
            sp.wait_ge(prep, 7)
            sp.dma_start(base_dram.rearrange("(p t) -> p t", p=HALF), g_base[:]).then_inc(base_out, 16)
            sp.dma_start(wide_dram.rearrange("(p t) -> p t", p=HALF), g_wide[:]).then_inc(base_out, 16)
            sp.wait_ge(base_out, 32)
            sp.dma_start(base_i, base_dram.rearrange("(o g) -> o g", o=1).broadcast_to([P, GROUPS])).then_inc(base_in, 16)
            sp.dma_start(wide_row, wide_dram.rearrange("(o g) -> o g", o=1)).then_inc(base_in, 16)
            for t, a in ((w_a, w0), (w_s, w_self)):
                sp.dma_start(t[:], a.rearrange("(k p) n -> p k n", p=P)).then_inc(w_in, 16)
            for t, a in ((bias[0], b0), (bias[1], b1)):
                sp.dma_start(t[:], a.rearrange("(o n) -> o n", o=1)).then_inc(w_in, 16)

            def source_round(r, first, last):
                for g in range(RING):
                    G, q = r * RING + g, g % SEL
                    if not (first and g < SEL):
                        sp.wait_ge(to_ready, G - SEL + 1)
                    sp.dma_start(src_all[:, q, :], src_n[bass.ds(G, 1), :].broadcast_to([P, GE])).then_inc(src_all_in[q], 16)

            rounds(sp, source_round)

            def store(l, i, q):
                d = dense[l]
                sp.wait_ge(d.normed, i + 1)
                sp.dma_start((x1_dram, out)[l][bass.ds(i * P, P), :], xo[:, q, :]).then_inc(d.stored[q], 16)

            for m in range(MSG):
                sp.wait_ge(msg_added[m], 16 * (CHUNKS // MSG))
            d0 = dense[0]

            def load0(i, q):
                for k in range(ACCS):
                    sp.dma_start(accs[:, q, k * D:(k + 1) * D], acc_tensors[k][bass.ds(i * P, P), :]).then_inc(accs_in[q], 16)
                sp.dma_start(xin[:, q, :], x[bass.ds(i * P, P), :]).then_inc(d0.xin_ready[q], 16)

            def step0(i, q, first, ahead):
                if ahead == 2:
                    sp.wait_ge(d0.y_ready, i + 1)
                    load0(i + 2, q)
                store(0, i, q)

            load0(0, 0)
            load0(1, 1)
            block_steps(sp, step0)
            sp.dma_start(w_a[:], w_neigh.rearrange("(k p) n -> p k n", p=P)).then_inc(wn_in, 16)
            sp.wait_ge(layer_summed, 1)
            all_stored(sp, d0)
            d1 = dense[1]

            def load1(i, q):
                sp.dma_start(xin[:, q, :], x1_dram[bass.ds(i * P, P), :]).then_inc(d1.xin_ready[q], 16)

            def step1(i, q, first, ahead):
                if ahead == 2:
                    sp.wait_ge(d1.y_ready, i + 1)
                    load1(i + 2, q)
                store(1, i, q)

            load1(0, 0)
            load1(1, 1)
            block_steps(sp, step1)
            all_stored(sp, d1)

        @block.gpsimd
        def _(pool):
            nc.gpsimd.iota(col_i, pattern=[[1, P]], base=0, channel_multiplier=0).then_inc(iotas, 1)
            nc.gpsimd.iota(par_i[:], pattern=[[0, 1]], base=0, channel_multiplier=1).then_inc(iotas, 1)

            def gather(table, sems, g, c):
                nc.gpsimd.indirect_dma_start(
                    gathered[:, g * GROUP + c, :], None, table,
                    bass.IndirectOffsetOnAxis(idx_now[g][:, c:c + 1].bitcast(U32), axis=0),
                ).then_inc(sems[g * GROUP + c], 16)

            pool.wait_ge(flag_ready, 1)
            wide = general(pool)

            def gather0(r, g, first):
                G = r * RING + g
                if not first:
                    pool.wait_ge(msg_summed, (G - RING + 1) * GROUP)
                pool.wait_ge(idx0_ready, G + 1)
                alone(pool)
                for c in range(GROUP):
                    gather(x, rows0_in, g, c)

            def add0(r, g, first):
                G = r * RING + g
                pool.wait_ge(to_ready, G + 1)
                for c in range(GROUP):
                    m, before = g % 2 * GROUP + c, (g % 2 * GROUP + c + MSG - ACCS) % MSG
                    turn = r * (RING // 2) + g // 2
                    pool.wait_ge(msg_ready, G * GROUP + c + 1)
                    if m >= ACCS:
                        pool.wait_ge(msg_added[before], 16 * (turn + 1))
                    elif not (first and g < 2):
                        pool.wait_ge(msg_added[before], 16 * turn)
                    alone(pool)
                    nc.gpsimd.indirect_dma_start(
                        acc_tensors[c],
                        bass.IndirectOffsetOnAxis(to_now[g][:, c:c + 1].bitcast(U32), axis=0),
                        msg[:, m, :], None, compute_op=ALU.add,
                    ).then_inc(msg_added[m], 16)

            pool.wait_ge(acc_zero, 16 * ACCS)
            for g in range(LEAD):
                gather0(0, g, True)

            def round0(r, first, last):
                for g in range(RING):
                    if g + LEAD < RING:
                        gather0(r, g + LEAD, first)
                    elif not last:
                        gather0(r + 1, g + LEAD - RING, False)
                    add0(r, g, first)

            rounds(pool, round0)
            all_stored(pool, dense[0])
            with pool.If(wide == 0):
                def gather_round(r, first, last):
                    for g in range(RING):
                        if not first:
                            pool.wait_ge(summed, (r - 1) * RING + g + 1)
                        pool.wait_ge(idx_ready, r * RING + g + 1)
                        alone(pool)
                        for c in range(GROUP):
                            gather(x1_dram, rows_in, g, c)

                rounds(pool, gather_round)
            with pool.Else():
                def gather_group(G, first):
                    if not first:
                        pool.wait_ge(summed, G * BLOCKS)
                    pool.wait_ge(idx_ready, G + 1)
                    alone(pool)
                    for c in range(GROUP):
                        gather(x1_dram, rows_in, 0, c)

                gather_group(0, True)
                with pool.Fori(1, GROUPS) as G:
                    gather_group(G, False)

        @block.scalar
        def _(act):
            act.wait_ge(flag_ready, 1)
            wide = general(act)

            def place0(r, g, first):
                G = r * RING + g
                if not first:
                    act.wait_ge(msg_summed, (G - RING + 1) * GROUP)
                nc.scalar.copy(idx_now[g][:], gat_all[:, bass.ds(G * GROUP, GROUP)]).then_inc(idx0_ready, 1)

            def evict0(r, g, first):
                G = r * RING + g
                for c in range(GROUP):
                    m = g % 2 * GROUP + c
                    act.wait_ge(msg_summed, G * GROUP + c + 1)
                    if not (first and g < 2):
                        act.wait_ge(msg_added[m], 16 * (r * (RING // 2) + g // 2))
                    nc.scalar.activation(msg[:, m, :], psum_msg[c][:], ACT.Copy).then_inc(msg_ready, 1)

            for g in range(RING - 1):
                place0(0, g, True)

            def round0(r, first, last):
                for g in range(RING):
                    if g == 0:
                        place0(r, RING - 1, first)
                    elif not last:
                        place0(r + 1, g - 1, False)
                    evict0(r, g, first)

            rounds(act, round0)

            def transposes_out(l, i, q, first):
                d = dense[l]
                act.wait_ge(d.transposed, i + 1)
                if not first:
                    act.wait_ge(d.projected, i - 1)
                last = nc.scalar.activation(agg_t[:, q, :, :], psum_t[:].rearrange("p (k n) -> p k n", k=KT), ACT.Copy)
                if l == 1:
                    last = nc.scalar.activation(x_t[:, q, :, :], psum_xt[:].rearrange("p (k n) -> p k n", k=KT), ACT.Copy)
                last.then_inc(d.t_ready, 1)

            def norm(l, i, q, first):
                d = dense[l]
                act.wait_ge(d.var_ready, i + 1)
                nc.scalar.activation(std[:, q, :], mv[:, q, 1:2], ACT.Sqrt, bias=eps[:]).then_inc(d.std_ready, 1)
                act.wait_ge(d.norm_ready, i + 1)
                if not first:
                    act.wait_ge(d.stored[q], 16 * half(i, q))
                nc.scalar.activation(xo[:, q, :], y[:, q, :], ACT.Identity, bias=shift[:, q, :],
                                     scale=rstd[:, q, :]).then_inc(d.normed, 1)

            def step0(i, q, first, ahead):
                if ahead:
                    transposes_out(0, i + 1, 1 - q, first and q == 0)
                norm(0, i, q, first)

            transposes_out(0, 0, 0, True)
            block_steps(act, step0)
            with act.If(wide == 0):
                def place_round(r, first, last):
                    for g in range(RING):
                        if not first:
                            act.wait_ge(summed, (r - 1) * RING + g + 1)
                        nc.scalar.copy(idx_now[g][:], idx_all[:, bass.ds((r * RING + g) * GROUP, GROUP)]).then_inc(idx_ready, 1)

                rounds(act, place_round)
            with act.Else():
                def place_group(G, first):
                    if not first:
                        act.wait_ge(summed, G * BLOCKS)
                    nc.scalar.copy(idx_now[0][:], idx_all[:, bass.ds(G * GROUP, GROUP)]).then_inc(idx_ready, 1)

                place_group(0, True)
                with act.Fori(1, GROUPS) as G:
                    place_group(G, False)
            d1 = dense[1]
            act.wait_ge(layer_summed, 1)
            all_stored(act, dense[0])

            def stage(i, q, first):
                act.wait_ge(rdeg_ready, i + 1)
                if not first:
                    act.wait_ge(d1.transposed, i - 1)
                nc.scalar.activation(staged[:, q, :], row_of(agg, i), ACT.Copy, scale=rdeg[:, q, :]).then_inc(d1.staged, 1)

            def step1(i, q, first, ahead):
                if ahead == 2:
                    stage(i + 2, q, False)
                if ahead:
                    transposes_out(1, i + 1, 1 - q, first and q == 0)
                norm(1, i, q, first)

            stage(0, 0, True)
            stage(1, 1, True)
            transposes_out(1, 0, 0, True)
            block_steps(act, step1)

        @block.vector
        def _(dve):
            steps = [0]

            def then(ins):
                steps[0] += 1
                ins.then_inc(prep, 1)
                dve.wait_ge(prep, steps[0])

            nc.vector.memset(zeros[:], 0.0).then_inc(zeros_ready, 1)
            dve.wait_ge(dstn_in, 16)
            then(nc.vector.tensor_copy(dn_f, dn_i))
            nc.vector.tensor_reduce(g_max[:], dn_f, AX.X, ALU.max)
            then(nc.vector.tensor_scalar(dn_pad, dn_f, 0.0, FAR, ALU.is_lt, ALU.mult))
            then(nc.vector.tensor_tensor(dn_pad, dn_pad, dn_f, ALU.add))
            then(nc.vector.tensor_reduce(g_min[:], dn_pad, AX.X, ALU.min))
            then(nc.vector.tensor_scalar(g_min[:], g_min[:], float(rows - 1), None, ALU.min))
            nc.vector.tensor_copy(g_base[:], g_min[:])
            then(nc.vector.tensor_tensor(g_wide_f[:], g_max[:], g_min[:], ALU.subtract))
            nc.vector.tensor_scalar(g_wide[:], g_wide_f[:], float(P), None, ALU.is_ge).then_inc(prep, 1)
            steps[0] += 1
            nc.vector.memset(ones[:], 1.0)
            nc.vector.memset(eps[:], EPS)
            then(nc.vector.memset(deg[:], 0.0))
            nc.vector.tensor_copy(ones_r[:], ones[:, 0:2])
            dve.wait_ge(iotas, 2)
            nc.vector.tensor_copy(col_f[:], col_i)
            then(nc.vector.tensor_copy(par_f[:], par_i[:]))
            nc.vector.tensor_scalar(ident[:], col_f[:], par_f[:], None, ALU.is_equal)
            nc.vector.tensor_scalar(tri[:], col_f[:], par_f[:], None, ALU.is_lt)
            nc.vector.tensor_scalar(spare_row, par_f[:], float(rows), None, ALU.add)
            dve.wait_ge(edges_in, 48)
            nc.vector.tensor_copy(dst_f[:], dst_i)
            nc.vector.tensor_copy(src_f, idx_all[:])
            then(nc.vector.tensor_scalar(row_i, dst_i, P - 1, None, ALU.bitwise_and))
            nc.vector.tensor_scalar(spare_f, src_f, -1.0, spare_row, ALU.mult, ALU.add)
            nc.vector.tensor_scalar(gat_all, dst_f[:], 0.0, None, ALU.max)
            nc.vector.tensor_copy(row_f[:], row_i)
            then(nc.vector.tensor_scalar(pad_f, dst_f[:], 0.0, NO_ROW, ALU.is_lt, ALU.mult))
            then(nc.vector.tensor_tensor(row_f[:], row_f[:], pad_f, ALU.add))
            dve.wait_ge(base_in, 32)
            nc.vector.tensor_scalar(blk_i[:], base_i[0:1, :], 7, None, ALU.logical_shift_right)
            then(nc.vector.tensor_scalar(brow_i, base_i, P - 1, None, ALU.bitwise_and))
            then(nc.vector.tensor_copy(brow_f, brow_i))
            then(nc.vector.tensor_scalar(in_lo[:], brow_f, par_f[:], None, ALU.is_le))
            nc.vector.tensor_scalar(in_hi[:], in_lo[:], -1.0, 1.0, ALU.mult, ALU.add)
            then(nc.vector.tensor_copy(wide_f, wide_row))
            then(nc.vector.tensor_reduce(any_f[:], wide_f, AX.X, ALU.max))
            nc.vector.tensor_copy(any_wide[:], any_f[:]).then_inc(flag_ready, 1)
            dve.wait_ge(flag_ready, 1)
            wide = general(dve)

            def match_round(r, first, last):
                for g in range(RING):
                    G, q = r * RING + g, g % SEL
                    turn = r * (RING // 2) + g // 2
                    dve.wait_ge(src_all_in[q], 16 * (turn + 1))
                    if not (first and g < SEL):
                        dve.wait_ge(msg_summed, (G - SEL + 1) * GROUP)
                    for c in range(GROUP):
                        col = G * GROUP + c
                        last_op = nc.vector.tensor_scalar(same[:, q, c, :], src_all[:, q, c * P:(c + 1) * P],
                                                          src_f[:, bass.ds(col, 1)], wgt[:, bass.ds(col, 1)],
                                                          ALU.is_equal, ALU.mult)
                    last_op.then_inc(same_ready, 1)
                    if not (first and g == 0):
                        dve.wait_ge(counted, G)
                    for c in range(GROUP):
                        last_op = nc.vector.scalar_tensor_tensor(scratch[:, c, :], src_all[:, q, c * P:(c + 1) * P],
                                                                 src_f[:, bass.ds(G * GROUP + c, 1)], tri[:],
                                                                 ALU.is_equal, ALU.mult, accum_out=earlier[:, q, c:c + 1])
                    last_op.then_inc(counted, 1)
                    dve.wait_ge(counted, G + 1)
                    nc.vector.scalar_tensor_tensor(to_f[:, q, :], earlier[:, q, :], 0.5, spare_f[:, bass.ds(G * GROUP, GROUP)],
                                                   ALU.is_ge, ALU.mult).then_inc(aimed, 1)
                    dve.wait_ge(aimed, G + 1)
                    if not first:
                        for c in range(GROUP):
                            dve.wait_ge(msg_added[g % 2 * GROUP + c], 16 * (turn - 1))
                    nc.vector.tensor_tensor(to_now[g][:], to_f[:, q, :], src_f[:, bass.ds(G * GROUP, GROUP)],
                                            ALU.add).then_inc(to_ready, 1)

            rounds(dve, match_round)

            def sum_accs(i, q, first):
                dve.wait_ge(accs_in[q], 16 * ACCS * (half(i, q) + 1))
                nc.vector.tensor_tensor(accs[:, q, 0:D], accs[:, q, 0:D], accs[:, q, D:2 * D], ALU.add)
                nc.vector.tensor_tensor(accs[:, q, 2 * D:3 * D], accs[:, q, 2 * D:3 * D], accs[:, q, 3 * D:4 * D],
                                        ALU.add).then_inc(acc_sum, 1)
                dve.wait_ge(acc_sum, i + 1)
                if not first:
                    dve.wait_ge(dense[0].transposed, i - 1)
                nc.vector.tensor_tensor(staged[:, q, :], accs[:, q, 0:D], accs[:, q, 2 * D:3 * D],
                                        ALU.add).then_inc(dense[0].staged, 1)

            def one_over_deg(i, q, first):
                if not first:
                    dve.wait_ge(dense[1].staged, i - 1)
                nc.vector.tensor_scalar(deg1[:, q, :], deg[:, bass.ds(i, 1)], 1.0, None, ALU.max).then_inc(deg1_ready, 1)
                dve.wait_ge(deg1_ready, i + 1)
                nc.vector.reciprocal(rdeg[:, q, :], deg1[:, q, :]).then_inc(rdeg_ready, 1)

            def moments(l, i, q, first):
                d = dense[l]
                dve.wait_ge(d.projected, i + 1)
                dve.wait_ge(d.xin_ready[q], 16 * (half(i, q) + 1))
                if not first:
                    dve.wait_ge(d.normed, i - 1)
                if l == 0:
                    nc.vector.tensor_tensor(y[:, q, :], psum_y[:], xin[:, q, :], ALU.add).then_inc(d.y_ready, 1)
                else:
                    nc.vector.scalar_tensor_tensor(y[:, q, :], psum_y[:], 0.0, xin[:, q, :], ALU.max, ALU.add).then_inc(d.y_ready, 1)
                dve.wait_ge(d.y_ready, i + 1)
                nc.vector.bn_stats(stats[:, q, :], y[:, q, :]).then_inc(d.stat, 1)
                dve.wait_ge(d.stat, i + 1)
                alone(dve)
                nc.vector.bn_aggr(mv[:, q, :], stats[:, q, :]).then_inc(d.var_ready, 1)

            def scales(l, i, q):
                d = dense[l]
                dve.wait_ge(d.std_ready, i + 1)
                nc.vector.reciprocal(rstd[:, q, :], std[:, q, :]).then_inc(d.rstd_ready, 1)
                dve.wait_ge(d.rstd_ready, i + 1)
                nc.vector.scalar_tensor_tensor(shift[:, q, :], mv[:, q, 0:1], -1.0, rstd[:, q, :], ALU.mult, ALU.mult
                                               ).then_inc(d.norm_ready, 1)

            def dense_steps(l, prepare):
                def step(i, q, first, ahead):
                    moments(l, i, q, first)
                    if ahead == 2:
                        prepare(i + 2, q, False)
                    scales(l, i, q)

                prepare(0, 0, True)
                prepare(1, 1, True)
                block_steps(dve, step)

            dense_steps(0, sum_accs)
            dve.wait_ge(dense[0].normed, BLOCKS)
            nc.vector.memset(agg[:], 0.0).then_inc(agg_zero, 1)
            dve.wait_ge(agg_zero, 1)
            with dve.If(wide == 0):
                def select(r, g, first):
                    q, G = g % SEL, r * RING + g
                    if not (first and g < SEL):
                        dve.wait_ge(summed, G - SEL + 1)
                    for c in range(GROUP):
                        last = nc.vector.tensor_scalar(sel[:, q, c, :], col_f[:], row_f[:, bass.ds(G * GROUP + c, 1)],
                                                       None, ALU.is_equal)
                    last.then_inc(sel_ready, 1)

                def add(G, g, first):
                    q = g % SEL
                    b = dve.value_load(blk_i[0:1, bass.ds(G, 1)], min_val=0, max_val=BLOCKS - 1)
                    dve.wait_ge(summed, G + 1)
                    if not first:
                        dve.wait_ge(added, G)
                    for at, mask in ((b, in_lo), (b + 1, in_hi)):
                        m = mask[:, bass.ds(G, 1)]
                        nc.vector.scalar_tensor_tensor(deg[:, bass.ds(at, 1)], psum_deg[q][:, 0:1], m,
                                                       deg[:, bass.ds(at, 1)], ALU.mult, ALU.add)
                        last = nc.vector.scalar_tensor_tensor(row_of(agg, at), psum_sum[q][:], m, row_of(agg, at),
                                                              ALU.mult, ALU.add)
                    last.then_inc(added, 1)

                def sum_round(r, first, last):
                    for g in range(RING):
                        select(r, g, first)
                        if not (first and g == 0):
                            add(r * RING + g - 1, g - 1, first and g == 1)

                rounds(dve, sum_round)
                add(GROUPS - 1, RING - 1, False)
            with dve.Else():
                nc.vector.memset(far_dst[:], 0.0).then_inc(added, 1)
                with dve.Fori(0, GROUPS) as G:
                    dve.wait_ge(added, G * (BLOCKS + 1) + 1)
                    nc.vector.tensor_copy(far_dst[:], dst_f[:, bass.ds(G * GROUP, GROUP)]).then_inc(added, 1)
                    with dve.Fori(0, BLOCKS) as b:
                        dve.wait_ge(added, G * (BLOCKS + 1) + b + 2)
                        for c in range(GROUP):
                            last = nc.vector.tensor_scalar(sel[:, 0, c, :], col_f[:], far_dst[:, c:c + 1], None, ALU.is_equal)
                        last.then_inc(sel_ready, 1)
                        dve.wait_ge(summed, G * BLOCKS + b + 1)
                        nc.vector.tensor_tensor(row_of(agg, b), psum_sum[0][:], row_of(agg, b), ALU.add)
                        nc.vector.tensor_tensor(deg[:, bass.ds(b, 1)], psum_deg[0][:, 0:1], deg[:, bass.ds(b, 1)], ALU.add)
                        nc.vector.tensor_scalar(far_dst[:], far_dst[:], float(P), None, ALU.subtract).then_inc(added, 1)
            dve.drain().then_inc(layer_summed, 1)
            dve.wait_ge(layer_summed, 1)
            dense_steps(1, one_over_deg)

        @block.tensor
        def _(pe):
            pe.wait_ge(flag_ready, 1)
            pe.wait_ge(w_in, 64)
            wide = general(pe)

            def message_round(r, first, last):
                for g in range(RING):
                    G = r * RING + g
                    pe.wait_ge(same_ready, G + 1)
                    for c in range(GROUP):
                        pe.wait_ge(rows0_in[g * GROUP + c], 16 * (r + 1))
                        if not (first and g == 0):
                            pe.wait_ge(msg_ready, (G - 1) * GROUP + c + 1)
                        nc.tensor.matmul(psum_msg[c][:], same[:, g % SEL, c, :], gathered[:, g * GROUP + c, :],
                                         start=True, stop=True).then_inc(msg_summed, 1)

            rounds(pe, message_round)

            def transposes(l, i, q, first):
                d = dense[l]
                pe.wait_ge(d.staged, i + 1)
                if not first:
                    pe.wait_ge(d.t_ready, i)
                for k in range(KT):
                    last = nc.tensor.transpose(psum_t[:, k * P:(k + 1) * P], staged[:, q, k * P:(k + 1) * P], ident[:])
                if l == 1:
                    pe.wait_ge(d.xin_ready[q], 16 * (half(i, q) + 1))
                    for k in range(KT):
                        last = nc.tensor.transpose(psum_xt[:, k * P:(k + 1) * P], xin[:, q, k * P:(k + 1) * P], ident[:])
                last.then_inc(d.transposed, 1)

            def project(l, i, q, first):
                d = dense[l]
                pe.wait_ge(d.t_ready, i + 1)
                if not first:
                    pe.wait_ge(d.y_ready, i)
                nc.tensor.matmul(psum_y[:], ones[0:1, :], bias[l][:], start=True, stop=False)
                pairs = [(agg_t, w_a)] if l == 0 else [(x_t, w_s), (agg_t, w_a)]
                for n, (a, w) in enumerate(pairs):
                    for k in range(KT):
                        last = nc.tensor.matmul(psum_y[:], a[:, q, k, :], w[:, k, :], start=False,
                                                stop=n == len(pairs) - 1 and k == KT - 1)
                last.then_inc(d.projected, 1)

            def dense_steps(l):
                def step(i, q, first, ahead):
                    if ahead:
                        transposes(l, i + 1, 1 - q, False)
                    project(l, i, q, first and q == 0)

                transposes(l, 0, 0, True)
                block_steps(pe, step)

            dense_steps(0)

            def sum_group(g, q):
                for c in range(GROUP):
                    nc.tensor.matmul(psum_sum[q][:], sel[:, q, c, :].bitcast(F32), gathered[:, g * GROUP + c, :],
                                     start=c == 0, stop=c == GROUP - 1)
                for c in range(GROUP):
                    last = nc.tensor.matmul(psum_deg[q][:, 0:2], sel[:, q, c, :], ones_r[:],
                                            start=c == 0, stop=c == GROUP - 1)
                last.then_inc(summed, 1)

            with pe.If(wide == 0):
                def sum_round(r, first, last):
                    for g in range(RING):
                        G = r * RING + g
                        pe.wait_ge(sel_ready, G + 1)
                        if not (first and g < SEL):
                            pe.wait_ge(added, G - SEL + 1)
                        for c in range(GROUP):
                            pe.wait_ge(rows_in[g * GROUP + c], 16 * (r + 1))
                        sum_group(g, g % SEL)

                rounds(pe, sum_round)
            with pe.Else():
                with pe.Fori(0, GROUPS) as G:
                    with pe.Fori(0, BLOCKS) as b:
                        for c in range(GROUP):
                            pe.wait_ge(rows_in[c], 16 * (G + 1))
                        pe.wait_ge(sel_ready, G * BLOCKS + b + 1)
                        sum_group(0, 0)
            pe.wait_ge(wn_in, 16)
            dense_steps(1)


_ORDER = ["x", "src_t", "dst_t", "w_t", "src_n", "dst_n", "w0", "b0", "w_self", "w_neigh", "b1"]


def kernel(x, src, dst, edge_weight, L0_gnn_weight, L0_gnn_bias, L1_gnn_W_self, L1_gnn_W_neigh, L1_gnn_b):
    import numpy as np
    import concourse.bacc as bacc
    from concourse.bass_utils import run_bass_kernel_spmd

    x = np.asarray(x)
    n, D = x.shape
    E = np.asarray(src).shape[0]
    per_round = RING * GROUP * CHUNK
    total = -(-E // per_round) * per_round

    def padded(a, fill):
        a = np.asarray(a)
        return np.concatenate([a, np.full(total - E, fill, a.dtype)])

    src, dst, w = padded(src, 0), padded(dst, -1), padded(edge_weight, 0)
    blocks = -(-n // P) // 2 * 2 + 1
    arrays = {
        "x": np.concatenate([x, np.zeros((blocks * P - n, D), x.dtype)]),
        "src_t": src.reshape(-1, P).T, "dst_t": dst.reshape(-1, P).T, "w_t": w.reshape(-1, P).T,
        "src_n": src.reshape(-1, GROUP * CHUNK), "dst_n": dst.reshape(-1, GROUP * CHUNK),
        "w0": L0_gnn_weight, "b0": L0_gnn_bias,
        "w_self": np.asarray(L1_gnn_W_self).T, "w_neigh": np.asarray(L1_gnn_W_neigh).T, "b1": L1_gnn_b,
    }
    arrays = {k: np.ascontiguousarray(v) for k, v in arrays.items()}
    nc = bacc.Bacc("TRN2", target_bir_lowering=False, num_devices=1)
    aps = [nc.dram_tensor(f"in_{k}", arrays[k].shape, mybir.dt.from_np(arrays[k].dtype), kind="ExternalInput").ap()
           for k in _ORDER]
    out = nc.dram_tensor("out_0", (blocks * P, D), F32, kind="ExternalOutput").ap()
    gnn_two_layers(nc, *aps, out)
    r = run_bass_kernel_spmd(nc, [{f"in_{k}": arrays[k] for k in _ORDER}], core_ids=[0])
    return np.asarray(r.results[0]["out_0"])[:n]
```

```python
from contextlib import ExitStack

import concourse.bass as bass
from concourse import mybir

F32 = mybir.dt.float32
F32R = mybir.dt.float32r
BF16 = mybir.dt.bfloat16
I32 = mybir.dt.int32
U32 = mybir.dt.uint32
ALU = mybir.AluOpType
ACT = mybir.ActivationFunctionType
AX = mybir.AxisListType

P = 128
CHUNK = 128
GROUP = 4
RING = 4
SEL = 2
MSG = 2 * GROUP
ACCS = GROUP
LEAD = 2
EPS = 1e-5
NO_ROW = 1000.0
FAR = 8192.0


def gnn_two_layers(nc, x, src_t, dst_t, w_t, src_n, dst_n, w0, b0, w_self, w_neigh, b1, out):
    rows, D = x.shape
    BLOCKS = rows // P
    CHUNKS = src_t.shape[1]
    GROUPS = CHUNKS // GROUP
    ROUNDS = GROUPS // RING
    HALF = GROUPS // 2
    KT = D // P
    GE = GROUP * CHUNK
    assert BLOCKS % 2 == 1 and BLOCKS >= 5 and GROUPS % RING == 0 and ROUNDS >= 3

    x1_dram = nc.dram_tensor("x1_dram", [rows, D], F32).ap()
    acc_tensors = [nc.dram_tensor(f"acc{k}", [rows + P, D], F32).ap() for k in range(ACCS)]
    base_dram = nc.dram_tensor("base_dram", [GROUPS], I32).ap()
    wide_dram = nc.dram_tensor("wide_dram", [GROUPS], I32).ap()

    ctx = ExitStack()
    with ctx:
        def sb(name, shape, dt=F32):
            return ctx.enter_context(nc.sbuf_tensor(name, shape, dt))

        def ps(name):
            return ctx.enter_context(nc.psum_tensor(name, [P, 512], F32))

        def sem(name):
            return ctx.enter_context(nc.semaphore(name))

        def lender(flat):
            taken = [0]

            def lend(*shape, parts=P):
                n = 1
                for k in shape:
                    n *= k
                a = flat[0:parts, taken[0]:taken[0] + n]
                taken[0] += n
                assert taken[0] <= flat.shape[1]
                if len(shape) == 2:
                    a = a.rearrange("p (a b) -> p a b", a=shape[0])
                if len(shape) == 3:
                    a = a.rearrange("p (a b c) -> p a b c", a=shape[0], b=shape[1])
                return a

            return lend

        agg = sb("agg", [P, BLOCKS + 1, D])
        deg = sb("deg", [P, BLOCKS + 1])
        gathered = sb("gathered", [P, RING * GROUP, D])
        sel = sb("sel", [P, SEL, GROUP, P], F32R)
        idx_all = sb("idx_all", [P, CHUNKS], I32)
        idx_now = [sb(f"idx_now{g}", [P, GROUP], I32) for g in range(RING)]
        to_now = [sb(f"to_now{g}", [P, GROUP], I32) for g in range(RING)]
        dst_f = sb("dst_f", [P, CHUNKS])
        row_f = sb("row_f", [P, CHUNKS])
        in_lo = sb("in_lo", [P, GROUPS])
        in_hi = sb("in_hi", [P, GROUPS])
        blk_i = sb("blk_i", [1, GROUPS], I32)
        from_i = sb("from_i", [1, GROUPS], I32)
        any_f = sb("any_f", [1, 1])
        any_wide = sb("any_wide", [1, 1], I32)
        g_max = sb("g_max", [HALF, 2])
        g_min = sb("g_min", [HALF, 2])
        g_base = sb("g_base", [HALF, 2], I32)
        g_wide_f = sb("g_wide_f", [HALF, 2])
        g_wide = sb("g_wide", [HALF, 2], I32)
        col_f = sb("col_f", [P, P])
        par_i = sb("par_i", [P, 1], I32)
        par_f = sb("par_f", [P, 1])
        ident = sb("ident", [P, P])
        tri = sb("tri", [P, P])
        ones = sb("ones", [P, P])
        ones_r = sb("ones_r", [P, P], F32R)
        ones_b = sb("ones_b", [P, 2], BF16)
        zeros = sb("zeros", [P, D])
        eps = sb("eps", [P, 1])
        w_a = sb("w_a", [P, KT, D])
        w_s = sb("w_s", [P, KT, D])
        bias = [sb(f"bias{l}", [2, D], F32R) for l in range(2)]
        part = sb("part", [2, 2])
        far_dst = sb("far_dst", [P, GROUP])
        staged = sb("staged", [P, 2, D])
        xin = sb("xin", [P, 2, D])
        agg_t = sb("agg_t", [P, 2, KT, P])
        x_t = sb("x_t", [P, 2, KT, P])
        y = sb("y", [P, 2, D])
        xo = sb("xo", [P, 2, D])
        stats = sb("stats", [P, 2, 6])
        mv = sb("mv", [P, 2, 2])
        std = sb("std", [P, 2, 1])
        rstd = sb("rstd", [P, 2, 1])
        shift = sb("shift", [P, 2, 1])
        deg1 = sb("deg1", [P, 2, 1])
        rdeg = sb("rdeg", [P, 2, 1])

        lend = lender(gathered[:].rearrange("p a d -> p (a d)"))
        dn_i = lend(2, GE, parts=HALF).bitcast(I32)
        dn_f = lend(2, GE, parts=HALF)
        dn_pad = lend(2, GE, parts=HALF)
        dst_i = lend(CHUNKS).bitcast(I32)
        row_i = lend(CHUNKS).bitcast(I32)
        pad_f = lend(CHUNKS)
        gat_f = lend(CHUNKS)
        base_i = lend(GROUPS).bitcast(I32)
        base_f = lend(GROUPS)
        brow_i = lend(GROUPS).bitcast(I32)
        brow_f = lend(GROUPS)
        wide_row = lend(GROUPS, parts=1).bitcast(I32)
        wide_f = lend(GROUPS, parts=1)
        col_i = lend(P).bitcast(I32)

        lend = lender(agg[:].rearrange("p a d -> p (a d)"))
        msg = lend(MSG, D)
        same = lend(SEL, GROUP, P)
        src_all = lend(RING, GE).bitcast(I32)
        window = lend(RING, D)
        near = lend(SEL, GROUP, P)
        mix = lend(SEL, GE)
        dst_near = lend(CHUNKS)
        accs = lend(2, ACCS * D)
        scratch = lend(GROUP, P)
        src_f = lend(CHUNKS)
        spare_f = lend(CHUNKS)
        gat_all = lend(CHUNKS).bitcast(I32)
        wgt = lend(CHUNKS)
        earlier = lend(SEL, GROUP)
        to_f = lend(SEL, GROUP)
        spare_row = lend(1)
        bias_in = lend(2, D, parts=2)
        bias_hi = lend(2, D, parts=2).bitcast(F32R)
        bias_lo = lend(2, D, parts=2)

        banks = [ps(f"bank{k}") for k in range(8)]
        psum_msg = banks[0:GROUP]
        psum_mix = banks[GROUP:GROUP + SEL]
        psum_sum = banks[0:SEL]
        psum_deg = banks[SEL:2 * SEL]
        psum_t, psum_xt = banks[4:6]
        psum_y = banks[6:8]

        edges_in = sem("edges_in")
        dstn_in = sem("dstn_in")
        w_in = sem("w_in")
        wn_in = sem("wn_in")
        base_out = sem("base_out")
        base_in = sem("base_in")
        iotas = sem("iotas")
        prep = sem("prep")
        zeros_ready = sem("zeros_ready")
        acc_zero = sem("acc_zero")
        flag_ready = sem("flag_ready")
        agg_zero = sem("agg_zero")
        waited = sem("waited")
        layer_summed = sem("layer_summed")

        idx0_ready = sem("idx0_ready")
        rows0_in = [sem(f"rows0_in{k}") for k in range(RING * GROUP)]
        src_all_in = [sem(f"src_all_in{g}") for g in range(RING)]
        window_in = [sem(f"window_in{g}") for g in range(RING)]
        mix_summed = sem("mix_summed")
        mix_ready = sem("mix_ready")
        same_ready = sem("same_ready")
        counted = sem("counted")
        aimed = sem("aimed")
        to_ready = sem("to_ready")
        msg_summed = sem("msg_summed")
        msg_ready = sem("msg_ready")
        msg_added = [sem(f"msg_added{m}") for m in range(MSG)]
        idx_ready = sem("idx_ready")
        rows_in = [sem(f"rows_in{k}") for k in range(RING * GROUP)]
        sel_ready = sem("sel_ready")
        summed = sem("summed")
        added = sem("added")

        class Dense:
            def __init__(self, l):
                self.xin_ready = [sem(f"xin_ready{l}{q}") for q in range(2)]
                self.staged = sem(f"staged{l}")
                self.transposed = sem(f"transposed{l}")
                self.t_ready = sem(f"t_ready{l}")
                self.projected = sem(f"projected{l}")
                self.y_ready = sem(f"y_ready{l}")
                self.stat = sem(f"stat{l}")
                self.var_ready = sem(f"var_ready{l}")
                self.std_ready = sem(f"std_ready{l}")
                self.rstd_ready = sem(f"rstd_ready{l}")
                self.norm_ready = sem(f"norm_ready{l}")
                self.normed = sem(f"normed{l}")
                self.stored = [sem(f"stored{l}{q}") for q in range(2)]

        dense = [Dense(l) for l in range(2)]
        accs_in = [sem(f"accs_in{q}") for q in range(2)]
        acc_sum = sem("acc_sum")
        deg1_ready = sem("deg1_ready")
        rdeg_ready = sem("rdeg_ready")

        def row_of(t, b):
            return t[:, b, :] if isinstance(b, int) else t[:, bass.ds(b, 1), :].rearrange("p o d -> p (o d)")

        def general(eng):
            return eng.value_load(any_wide[0:1, 0:1], min_val=0, max_val=1)

        def alone(eng):
            eng.sem_inc(waited, 1)

        def rounds(eng, one_round):
            one_round(0, True, False)
            with eng.Fori(1, ROUNDS - 1) as r:
                one_round(r, False, False)
            one_round(ROUNDS - 1, False, True)

        def block_steps(eng, step):
            step(0, 0, True, 2)
            step(1, 1, True, 2)
            step(2, 0, False, 2)
            with eng.Fori(3, BLOCKS - 3, 2) as i:
                step(i, 1, False, 2)
                step(i + 1, 0, False, 2)
            step(BLOCKS - 2, 1, False, 1)
            step(BLOCKS - 1, 0, False, 0)

        def half(i, q):
            return (i - q) // 2

        def all_stored(eng, d):
            eng.wait_ge(d.stored[0], 16 * (BLOCKS // 2 + 1))
            eng.wait_ge(d.stored[1], 16 * (BLOCKS // 2))

        block = ctx.enter_context(nc.Block())

        @block.sync
        def _(sp):
            sp.dma_start(dn_i, dst_n.rearrange("(p t) e -> p t e", p=HALF)).then_inc(dstn_in, 16)
            for t, a in ((idx_all[:], src_t), (dst_i, dst_t), (wgt, w_t)):
                sp.dma_start(t, a).then_inc(edges_in, 16)
            for l, a in enumerate((b0, b1)):
                sp.dma_start(bias_in[:, l, :], a.rearrange("(o n) -> o n", o=1).broadcast_to([2, D])).then_inc(edges_in, 16)
            sp.wait_ge(zeros_ready, 1)
            for k in range(ACCS):
                sp.dma_start(acc_tensors[k].rearrange("(b p) d -> p b d", p=P),
                             zeros[:].rearrange("p (o d) -> p o d", o=1).broadcast_to([P, BLOCKS + 1, D])).then_inc(acc_zero, 16)
            sp.wait_ge(prep, 7)
            sp.dma_start(base_dram.rearrange("(p t) -> p t", p=HALF), g_base[:]).then_inc(base_out, 16)
            sp.dma_start(wide_dram.rearrange("(p t) -> p t", p=HALF), g_wide[:]).then_inc(base_out, 16)
            sp.wait_ge(base_out, 32)
            sp.dma_start(base_i, base_dram.rearrange("(o g) -> o g", o=1).broadcast_to([P, GROUPS])).then_inc(base_in, 16)
            sp.dma_start(wide_row, wide_dram.rearrange("(o g) -> o g", o=1)).then_inc(base_in, 16)
            for t, a in ((w_a, w0), (w_s, w_self)):
                sp.dma_start(t[:], a.rearrange("(k p) n -> p k n", p=P)).then_inc(w_in, 16)

            sp.wait_ge(flag_ready, 1)
            wide = general(sp)

            def source_rounds(windows):
                def source_round(r, first, last):
                    for g in range(RING):
                        G = r * RING + g
                        if not first:
                            sp.wait_ge(to_ready, G - RING + 1)
                        sp.dma_start(src_all[:, g, :], src_n[bass.ds(G, 1), :].broadcast_to([P, GE])).then_inc(src_all_in[g], 16)
                        if windows:
                            v = sp.value_load(from_i[0:1, bass.ds(G, 1)], min_val=0, max_val=rows - P)
                            if not first:
                                sp.wait_ge(msg_summed, (G - RING + 1) * GROUP)
                            sp.dma_start(window[:, g, :], x[bass.ds(v, P), :]).then_inc(window_in[g], 16)

                rounds(sp, source_round)

            with sp.If(wide == 0):
                source_rounds(True)
            with sp.Else():
                source_rounds(False)

            for m in range(MSG):
                sp.wait_ge(msg_added[m], 16 * (CHUNKS // MSG))
            d0 = dense[0]

            def load_accs(i, q):
                for k in range(ACCS):
                    sp.dma_start(accs[:, q, k * D:(k + 1) * D], acc_tensors[k][bass.ds(i * P, P), :]).then_inc(accs_in[q], 16)

            def load_x(i, q):
                sp.dma_start(xin[:, q, :], x[bass.ds(i * P, P), :]).then_inc(d0.xin_ready[q], 16)

            def step0(i, q, first, ahead):
                if ahead == 2:
                    sp.wait_ge(d0.staged, i + 1)
                    load_accs(i + 2, q)
                if ahead and not (first and q == 0):
                    sp.wait_ge(d0.y_ready, i)
                    load_x(i + 1, 1 - q)

            for i in range(2):
                load_accs(i, i)
                load_x(i, i)
            block_steps(sp, step0)
            sp.wait_ge(d0.projected, BLOCKS)
            sp.dma_start(w_a[:], w_neigh.rearrange("(k p) n -> p k n", p=P)).then_inc(wn_in, 16)
            sp.wait_ge(layer_summed, 1)
            all_stored(sp, d0)
            d1 = dense[1]

            def load1(i, q):
                sp.dma_start(xin[:, q, :], x1_dram[bass.ds(i * P, P), :]).then_inc(d1.xin_ready[q], 16)

            def step1(i, q, first, ahead):
                if ahead == 2:
                    sp.wait_ge(d1.y_ready, i + 1)
                    load1(i + 2, q)

            load1(0, 0)
            load1(1, 1)
            block_steps(sp, step1)
            all_stored(sp, d1)

        @block.gpsimd
        def _(pool):
            nc.gpsimd.iota(col_i, pattern=[[1, P]], base=0, channel_multiplier=0).then_inc(iotas, 1)
            nc.gpsimd.iota(par_i[:], pattern=[[0, 1]], base=0, channel_multiplier=1).then_inc(iotas, 1)

            def gather(table, sems, g, c):
                nc.gpsimd.indirect_dma_start(
                    gathered[:, g * GROUP + c, :], None, table,
                    bass.IndirectOffsetOnAxis(idx_now[g][:, c:c + 1].bitcast(U32), axis=0),
                ).then_inc(sems[g * GROUP + c], 16)

            pool.wait_ge(flag_ready, 1)
            wide = general(pool)

            def gather0(r, g, first):
                G = r * RING + g
                if not first:
                    pool.wait_ge(msg_summed, (G - RING + 1) * GROUP)
                pool.wait_ge(idx0_ready, G + 1)
                alone(pool)
                for c in range(GROUP):
                    gather(x, rows0_in, g, c)

            def add0(r, g, first):
                G = r * RING + g
                pool.wait_ge(to_ready, G + 1)
                for c in range(GROUP):
                    m, before = g % 2 * GROUP + c, (g % 2 * GROUP + c + MSG - ACCS) % MSG
                    turn = r * (RING // 2) + g // 2
                    pool.wait_ge(msg_ready, G * GROUP + c + 1)
                    if m >= ACCS:
                        pool.wait_ge(msg_added[before], 16 * (turn + 1))
                    elif not (first and g < 2):
                        pool.wait_ge(msg_added[before], 16 * turn)
                    alone(pool)
                    nc.gpsimd.indirect_dma_start(
                        acc_tensors[c],
                        bass.IndirectOffsetOnAxis(to_now[g][:, c:c + 1].bitcast(U32), axis=0),
                        msg[:, m, :], None, compute_op=ALU.add,
                    ).then_inc(msg_added[m], 16)

            pool.wait_ge(acc_zero, 16 * ACCS)
            with pool.If(wide == 0):
                def round0(r, first, last):
                    for g in range(RING):
                        add0(r, g, first)

                rounds(pool, round0)
            with pool.Else():
                for g in range(LEAD):
                    gather0(0, g, True)

                def round0(r, first, last):
                    for g in range(RING):
                        if g + LEAD < RING:
                            gather0(r, g + LEAD, first)
                        elif not last:
                            gather0(r + 1, g + LEAD - RING, False)
                        add0(r, g, first)

                rounds(pool, round0)
            all_stored(pool, dense[0])
            with pool.If(wide == 0):
                def gather_round(r, first, last):
                    for g in range(RING):
                        if not first:
                            pool.wait_ge(summed, (r - 1) * RING + g + 1)
                        pool.wait_ge(idx_ready, r * RING + g + 1)
                        alone(pool)
                        for c in range(GROUP):
                            gather(x1_dram, rows_in, g, c)

                rounds(pool, gather_round)
            with pool.Else():
                def gather_group(G, first):
                    if not first:
                        pool.wait_ge(summed, G * BLOCKS)
                    pool.wait_ge(idx_ready, G + 1)
                    alone(pool)
                    for c in range(GROUP):
                        gather(x1_dram, rows_in, 0, c)

                gather_group(0, True)
                with pool.Fori(1, GROUPS) as G:
                    gather_group(G, False)

        @block.scalar
        def _(act):
            act.wait_ge(flag_ready, 1)
            wide = general(act)

            def place0(r, g, first):
                G = r * RING + g
                if not first:
                    act.wait_ge(msg_summed, (G - RING + 1) * GROUP)
                nc.scalar.copy(idx_now[g][:], gat_all[:, bass.ds(G * GROUP, GROUP)]).then_inc(idx0_ready, 1)

            def evict0(r, g, first):
                G = r * RING + g
                for c in range(GROUP):
                    m = g % 2 * GROUP + c
                    act.wait_ge(msg_summed, G * GROUP + c + 1)
                    if not (first and g < 2):
                        act.wait_ge(msg_added[m], 16 * (r * (RING // 2) + g // 2))
                    nc.scalar.activation(msg[:, m, :], psum_msg[c][:], ACT.Copy).then_inc(msg_ready, 1)

            def mix_out(r, g, first):
                G = r * RING + g
                act.wait_ge(mix_summed, G + 1)
                if not (first and g < SEL):
                    act.wait_ge(msg_summed, (G - SEL + 1) * GROUP)
                nc.scalar.activation(mix[:, g % SEL, :], psum_mix[g % SEL][:], ACT.Copy).then_inc(mix_ready, 1)

            with act.If(wide == 0):
                def round0(r, first, last):
                    for g in range(RING):
                        if g + 1 < RING:
                            mix_out(r, g + 1, first)
                        elif not last:
                            mix_out(r + 1, 0, False)
                        evict0(r, g, first)

                mix_out(0, 0, True)
                rounds(act, round0)
            with act.Else():
                for g in range(RING - 1):
                    place0(0, g, True)

                def round0(r, first, last):
                    for g in range(RING):
                        if g == 0:
                            place0(r, RING - 1, first)
                        elif not last:
                            place0(r + 1, g - 1, False)
                        evict0(r, g, first)

                rounds(act, round0)

            def transposes_out(l, i, q, first):
                d = dense[l]
                act.wait_ge(d.transposed, i + 1)
                if not first:
                    act.wait_ge(d.projected, i - 1)
                last = nc.scalar.activation(agg_t[:, q, :, :], psum_t[:].rearrange("p (k n) -> p k n", k=KT), ACT.Copy)
                if l == 1:
                    last = nc.scalar.activation(x_t[:, q, :, :], psum_xt[:].rearrange("p (k n) -> p k n", k=KT), ACT.Copy)
                last.then_inc(d.t_ready, 1)

            def norm(l, i, q, first):
                d = dense[l]
                act.wait_ge(d.var_ready, i + 1)
                nc.scalar.activation(std[:, q, :], mv[:, q, 1:2], ACT.Sqrt, bias=eps[:]).then_inc(d.std_ready, 1)
                act.wait_ge(d.norm_ready, i + 1)
                if not first:
                    act.wait_ge(d.stored[q], 16 * half(i, q))
                nc.scalar.activation(xo[:, q, :], y[:, q, :], ACT.Identity, bias=shift[:, q, :],
                                     scale=rstd[:, q, :]).then_inc(d.normed, 1)

            def store(l, i, q):
                act.wait_ge(dense[l].normed, i + 1)
                act.dma_start((x1_dram, out)[l][bass.ds(i * P, P), :], xo[:, q, :]).then_inc(dense[l].stored[q], 16)

            def step0(i, q, first, ahead):
                if ahead:
                    transposes_out(0, i + 1, 1 - q, first and q == 0)
                if not (first and q == 0):
                    store(0, i - 1, 1 - q)
                norm(0, i, q, first)

            transposes_out(0, 0, 0, True)
            block_steps(act, step0)
            store(0, BLOCKS - 1, 0)
            with act.If(wide == 0):
                def place_round(r, first, last):
                    for g in range(RING):
                        if not first:
                            act.wait_ge(summed, (r - 1) * RING + g + 1)
                        nc.scalar.copy(idx_now[g][:], idx_all[:, bass.ds((r * RING + g) * GROUP, GROUP)]).then_inc(idx_ready, 1)

                rounds(act, place_round)
            with act.Else():
                def place_group(G, first):
                    if not first:
                        act.wait_ge(summed, G * BLOCKS)
                    nc.scalar.copy(idx_now[0][:], idx_all[:, bass.ds(G * GROUP, GROUP)]).then_inc(idx_ready, 1)

                place_group(0, True)
                with act.Fori(1, GROUPS) as G:
                    place_group(G, False)
            d1 = dense[1]
            act.wait_ge(layer_summed, 1)
            all_stored(act, dense[0])

            def stage(i, q, first):
                act.wait_ge(rdeg_ready, i + 1)
                if not first:
                    act.wait_ge(d1.transposed, i - 1)
                nc.scalar.activation(staged[:, q, :], row_of(agg, i), ACT.Copy, scale=rdeg[:, q, :]).then_inc(d1.staged, 1)

            def step1(i, q, first, ahead):
                if ahead:
                    transposes_out(1, i + 1, 1 - q, first and q == 0)
                if not (first and q == 0):
                    store(1, i - 1, 1 - q)
                if ahead == 2:
                    stage(i + 2, q, False)
                norm(1, i, q, first)

            stage(0, 0, True)
            stage(1, 1, True)
            transposes_out(1, 0, 0, True)
            block_steps(act, step1)
            store(1, BLOCKS - 1, 0)

        @block.vector
        def _(dve):
            steps = [0]

            def then(ins):
                steps[0] += 1
                ins.then_inc(prep, 1)
                dve.wait_ge(prep, steps[0])

            nc.vector.memset(zeros[:], 0.0).then_inc(zeros_ready, 1)
            dve.wait_ge(dstn_in, 16)
            then(nc.vector.tensor_copy(dn_f, dn_i))
            nc.vector.tensor_reduce(g_max[:], dn_f, AX.X, ALU.max)
            then(nc.vector.tensor_scalar(dn_pad, dn_f, 0.0, FAR, ALU.is_lt, ALU.mult))
            then(nc.vector.tensor_tensor(dn_pad, dn_pad, dn_f, ALU.add))
            then(nc.vector.tensor_reduce(g_min[:], dn_pad, AX.X, ALU.min))
            then(nc.vector.tensor_scalar(g_min[:], g_min[:], float(rows - P), None, ALU.min))
            nc.vector.tensor_copy(g_base[:], g_min[:])
            then(nc.vector.tensor_tensor(g_wide_f[:], g_max[:], g_min[:], ALU.subtract))
            nc.vector.tensor_scalar(g_wide[:], g_wide_f[:], float(P), None, ALU.is_ge).then_inc(prep, 1)
            steps[0] += 1
            nc.vector.memset(ones[:], 1.0)
            nc.vector.memset(eps[:], EPS)
            then(nc.vector.memset(deg[:], 0.0))
            nc.vector.tensor_copy(ones_r[:], ones[:])
            nc.vector.tensor_copy(ones_b[:], ones[:, 0:2])
            dve.wait_ge(iotas, 2)
            nc.vector.tensor_copy(col_f[:], col_i)
            then(nc.vector.tensor_copy(par_f[:], par_i[:]))
            nc.vector.tensor_scalar(ident[:], col_f[:], par_f[:], None, ALU.is_equal)
            nc.vector.tensor_scalar(tri[:], col_f[:], par_f[:], None, ALU.is_lt)
            nc.vector.tensor_scalar(spare_row, par_f[:], float(rows), None, ALU.add)
            dve.wait_ge(edges_in, 80)
            nc.vector.tensor_copy(dst_f[:], dst_i)
            nc.vector.tensor_copy(src_f, idx_all[:])
            then(nc.vector.tensor_scalar(row_i, dst_i, P - 1, None, ALU.bitwise_and))
            nc.vector.tensor_scalar(spare_f, src_f, -1.0, spare_row, ALU.mult, ALU.add)
            nc.vector.tensor_scalar(gat_all, dst_f[:], 0.0, None, ALU.max)
            nc.vector.tensor_copy(row_f[:], row_i)
            then(nc.vector.tensor_scalar(pad_f, dst_f[:], 0.0, NO_ROW, ALU.is_lt, ALU.mult))
            then(nc.vector.tensor_tensor(row_f[:], row_f[:], pad_f, ALU.add))
            nc.vector.tensor_scalar(part[:, 0:1], par_f[0:2, :], 0.0, None, ALU.is_equal)
            nc.vector.tensor_scalar(part[:, 1:2], par_f[0:2, :], 1.0, None, ALU.is_equal)
            then(nc.vector.tensor_copy(bias_hi, bias_in))
            then(nc.vector.tensor_tensor(bias_lo, bias_in, bias_hi.bitcast(F32), ALU.subtract))
            then(nc.vector.tensor_scalar(bias_lo, bias_lo, part[:, 1:2], None, ALU.mult))
            for l in range(2):
                nc.vector.scalar_tensor_tensor(bias[l][:], bias_hi[:, l, :].bitcast(F32), part[:, 0:1], bias_lo[:, l, :], ALU.mult, ALU.add)
            dve.wait_ge(base_in, 32)
            nc.vector.tensor_copy(from_i[:], base_i[0:1, :])
            then(nc.vector.tensor_copy(base_f, base_i))
            nc.vector.tensor_tensor(dst_near.rearrange("p (g c) -> p g c", c=GROUP), dst_f[:].rearrange("p (g c) -> p g c", c=GROUP),
                                    base_f.rearrange("p (g o) -> p g o", o=1).broadcast_to([P, GROUPS, GROUP]), ALU.subtract)
            nc.vector.tensor_scalar(blk_i[:], base_i[0:1, :], 7, None, ALU.logical_shift_right)
            then(nc.vector.tensor_scalar(brow_i, base_i, P - 1, None, ALU.bitwise_and))
            then(nc.vector.tensor_copy(brow_f, brow_i))
            then(nc.vector.tensor_scalar(in_lo[:], brow_f, par_f[:], None, ALU.is_le))
            nc.vector.tensor_scalar(in_hi[:], in_lo[:], -1.0, 1.0, ALU.mult, ALU.add)
            then(nc.vector.tensor_copy(wide_f, wide_row))
            then(nc.vector.tensor_reduce(any_f[:], wide_f, AX.X, ALU.max))
            nc.vector.tensor_copy(any_wide[:], any_f[:]).then_inc(flag_ready, 1)
            dve.wait_ge(flag_ready, 1)
            wide = general(dve)

            def match_rounds(windows):
                def match_round(r, first, last):
                    for g in range(RING):
                        G, q = r * RING + g, g % SEL
                        turn = r * (RING // 2) + g // 2
                        if not (first and g < SEL):
                            if windows:
                                dve.wait_ge(mix_summed, G - SEL + 1)
                            else:
                                dve.wait_ge(msg_summed, (G - SEL + 1) * GROUP)
                        if windows:
                            nc.vector.tensor_tensor(near[:, q, :, :], col_f[:].rearrange("p (o m) -> p o m", o=1).broadcast_to([P, GROUP, P]),
                                                    dst_near[:, bass.ds(G * GROUP, GROUP)].rearrange("p (c o) -> p c o", o=1).broadcast_to([P, GROUP, P]),
                                                    ALU.is_equal)
                        dve.wait_ge(src_all_in[g], 16 * (r + 1))
                        for c in range(GROUP):
                            col = G * GROUP + c
                            last_op = nc.vector.tensor_scalar(same[:, q, c, :], src_all[:, g, c * P:(c + 1) * P],
                                                              src_f[:, bass.ds(col, 1)], wgt[:, bass.ds(col, 1)],
                                                              ALU.is_equal, ALU.mult)
                        last_op.then_inc(same_ready, 1)
                        if not (first and g == 0):
                            dve.wait_ge(counted, G)
                        for c in range(GROUP):
                            last_op = nc.vector.scalar_tensor_tensor(scratch[:, c, :], src_all[:, g, c * P:(c + 1) * P],
                                                                     src_f[:, bass.ds(G * GROUP + c, 1)], tri[:],
                                                                     ALU.is_equal, ALU.mult, accum_out=earlier[:, q, c:c + 1])
                        last_op.then_inc(counted, 1)
                        dve.wait_ge(counted, G + 1)
                        nc.vector.scalar_tensor_tensor(to_f[:, q, :], earlier[:, q, :], 0.5, spare_f[:, bass.ds(G * GROUP, GROUP)],
                                                       ALU.is_ge, ALU.mult).then_inc(aimed, 1)
                        dve.wait_ge(aimed, G + 1)
                        if not first:
                            for c in range(GROUP):
                                dve.wait_ge(msg_added[g % 2 * GROUP + c], 16 * (turn - 1))
                        nc.vector.tensor_tensor(to_now[g][:], to_f[:, q, :], src_f[:, bass.ds(G * GROUP, GROUP)],
                                                ALU.add).then_inc(to_ready, 1)

                rounds(dve, match_round)

            with dve.If(wide == 0):
                match_rounds(True)
            with dve.Else():
                match_rounds(False)

            def sum_accs(i, q, first):
                dve.wait_ge(accs_in[q], 16 * ACCS * (half(i, q) + 1))
                nc.vector.tensor_tensor(accs[:, q, 0:D], accs[:, q, 0:D], accs[:, q, D:2 * D], ALU.add)
                nc.vector.tensor_tensor(accs[:, q, 2 * D:3 * D], accs[:, q, 2 * D:3 * D], accs[:, q, 3 * D:4 * D],
                                        ALU.add).then_inc(acc_sum, 1)
                dve.wait_ge(acc_sum, i + 1)
                if not first:
                    dve.wait_ge(dense[0].transposed, i - 1)
                nc.vector.tensor_tensor(staged[:, q, :], accs[:, q, 0:D], accs[:, q, 2 * D:3 * D],
                                        ALU.add).then_inc(dense[0].staged, 1)

            def one_over_deg(i, q, first):
                if not first:
                    dve.wait_ge(dense[1].staged, i - 1)
                nc.vector.tensor_scalar(deg1[:, q, :], deg[:, bass.ds(i, 1)], 1.0, None, ALU.max).then_inc(deg1_ready, 1)
                dve.wait_ge(deg1_ready, i + 1)
                nc.vector.reciprocal(rdeg[:, q, :], deg1[:, q, :]).then_inc(rdeg_ready, 1)

            def moments(l, i, q, first):
                d = dense[l]
                dve.wait_ge(d.projected, i + 1)
                dve.wait_ge(d.xin_ready[q], 16 * (half(i, q) + 1))
                if not first:
                    dve.wait_ge(d.normed, i - 1)
                if l == 0:
                    nc.vector.tensor_tensor(y[:, q, :], psum_y[q][:], xin[:, q, :], ALU.add).then_inc(d.y_ready, 1)
                else:
                    nc.vector.scalar_tensor_tensor(y[:, q, :], psum_y[q][:], 0.0, xin[:, q, :], ALU.max, ALU.add).then_inc(d.y_ready, 1)
                dve.wait_ge(d.y_ready, i + 1)
                nc.vector.bn_stats(stats[:, q, :], y[:, q, :]).then_inc(d.stat, 1)
                dve.wait_ge(d.stat, i + 1)
                alone(dve)
                nc.vector.bn_aggr(mv[:, q, :], stats[:, q, :]).then_inc(d.var_ready, 1)

            def scales(l, i, q):
                d = dense[l]
                dve.wait_ge(d.std_ready, i + 1)
                nc.vector.reciprocal(rstd[:, q, :], std[:, q, :]).then_inc(d.rstd_ready, 1)
                dve.wait_ge(d.rstd_ready, i + 1)
                nc.vector.scalar_tensor_tensor(shift[:, q, :], mv[:, q, 0:1], -1.0, rstd[:, q, :], ALU.mult, ALU.mult
                                               ).then_inc(d.norm_ready, 1)

            def dense_steps(l, prepare):
                def step(i, q, first, ahead):
                    if ahead == 2:
                        prepare(i + 2, q, False)
                    moments(l, i, q, first)
                    scales(l, i, q)

                prepare(0, 0, True)
                prepare(1, 1, True)
                block_steps(dve, step)

            dense_steps(0, sum_accs)
            dve.wait_ge(dense[0].normed, BLOCKS)
            nc.vector.memset(agg[:], 0.0).then_inc(agg_zero, 1)
            dve.wait_ge(agg_zero, 1)
            with dve.If(wide == 0):
                def select(r, g, first):
                    q, G = g % SEL, r * RING + g
                    if not (first and g < SEL):
                        dve.wait_ge(summed, G - SEL + 1)
                    for c in range(GROUP):
                        last = nc.vector.tensor_scalar(sel[:, q, c, :], col_f[:], row_f[:, bass.ds(G * GROUP + c, 1)],
                                                       None, ALU.is_equal)
                    last.then_inc(sel_ready, 1)

                def add(G, g, first):
                    q = g % SEL
                    b = dve.value_load(blk_i[0:1, bass.ds(G, 1)], min_val=0, max_val=BLOCKS - 1)
                    dve.wait_ge(summed, G + 1)
                    if not first:
                        dve.wait_ge(added, G)
                    for at, mask in ((b, in_lo), (b + 1, in_hi)):
                        m = mask[:, bass.ds(G, 1)]
                        nc.vector.scalar_tensor_tensor(deg[:, bass.ds(at, 1)], psum_deg[q][:, 0:1], m,
                                                       deg[:, bass.ds(at, 1)], ALU.mult, ALU.add)
                        last = nc.vector.scalar_tensor_tensor(row_of(agg, at), psum_sum[q][:], m, row_of(agg, at),
                                                              ALU.mult, ALU.add)
                    last.then_inc(added, 1)

                def sum_round(r, first, last):
                    for g in range(RING):
                        select(r, g, first)
                        if not (first and g == 0):
                            add(r * RING + g - 1, g - 1, first and g == 1)

                rounds(dve, sum_round)
                add(GROUPS - 1, RING - 1, False)
            with dve.Else():
                nc.vector.memset(far_dst[:], 0.0).then_inc(added, 1)
                with dve.Fori(0, GROUPS) as G:
                    dve.wait_ge(added, G * (BLOCKS + 1) + 1)
                    nc.vector.tensor_copy(far_dst[:], dst_f[:, bass.ds(G * GROUP, GROUP)]).then_inc(added, 1)
                    with dve.Fori(0, BLOCKS) as b:
                        dve.wait_ge(added, G * (BLOCKS + 1) + b + 2)
                        for c in range(GROUP):
                            last = nc.vector.tensor_scalar(sel[:, 0, c, :], col_f[:], far_dst[:, c:c + 1], None, ALU.is_equal)
                        last.then_inc(sel_ready, 1)
                        dve.wait_ge(summed, G * BLOCKS + b + 1)
                        nc.vector.tensor_tensor(row_of(agg, b), psum_sum[0][:], row_of(agg, b), ALU.add)
                        nc.vector.tensor_tensor(deg[:, bass.ds(b, 1)], psum_deg[0][:, 0:1], deg[:, bass.ds(b, 1)], ALU.add)
                        nc.vector.tensor_scalar(far_dst[:], far_dst[:], float(P), None, ALU.subtract).then_inc(added, 1)
            dve.drain().then_inc(layer_summed, 1)
            dve.wait_ge(layer_summed, 1)
            dense_steps(1, one_over_deg)

        @block.tensor
        def _(pe):
            pe.wait_ge(flag_ready, 1)
            pe.wait_ge(w_in, 32)
            wide = general(pe)

            def message(r, g, c, first, weights, table):
                if not (first and g == 0):
                    pe.wait_ge(msg_ready, (r * RING + g - 1) * GROUP + c + 1)
                nc.tensor.matmul(psum_msg[c][:], weights, table, start=True, stop=True).then_inc(msg_summed, 1)

            with pe.If(wide == 0):
                def mix_group(r, g, first):
                    G, q = r * RING + g, g % SEL
                    pe.wait_ge(same_ready, G + 1)
                    if not (first and g < SEL):
                        pe.wait_ge(mix_ready, G - SEL + 1)
                    for c in range(GROUP):
                        last = nc.tensor.matmul(psum_mix[q][:, c * P:(c + 1) * P], near[:, q, c, :], same[:, q, c, :],
                                                start=True, stop=True)
                    last.then_inc(mix_summed, 1)

                def message_round(r, first, last):
                    for g in range(RING):
                        G, q = r * RING + g, g % SEL
                        if g + 1 < RING:
                            mix_group(r, g + 1, first)
                        elif not last:
                            mix_group(r + 1, 0, False)
                        pe.wait_ge(mix_ready, G + 1)
                        pe.wait_ge(window_in[g], 16 * (r + 1))
                        for c in range(GROUP):
                            message(r, g, c, first, mix[:, q, c * P:(c + 1) * P], window[:, g, :])

                mix_group(0, 0, True)
                rounds(pe, message_round)
            with pe.Else():
                def message_round(r, first, last):
                    for g in range(RING):
                        pe.wait_ge(same_ready, r * RING + g + 1)
                        for c in range(GROUP):
                            pe.wait_ge(rows0_in[g * GROUP + c], 16 * (r + 1))
                            message(r, g, c, first, same[:, g % SEL, c, :], gathered[:, g * GROUP + c, :])

                rounds(pe, message_round)

            def transposes(l, i, q, first):
                d = dense[l]
                pe.wait_ge(d.staged, i + 1)
                if not first:
                    pe.wait_ge(d.t_ready, i)
                for k in range(KT):
                    last = nc.tensor.transpose(psum_t[:, k * P:(k + 1) * P], staged[:, q, k * P:(k + 1) * P], ident[:])
                if l == 1:
                    pe.wait_ge(d.xin_ready[q], 16 * (half(i, q) + 1))
                    for k in range(KT):
                        last = nc.tensor.transpose(psum_xt[:, k * P:(k + 1) * P], xin[:, q, k * P:(k + 1) * P], ident[:])
                last.then_inc(d.transposed, 1)

            def project(l, i, q, first):
                d = dense[l]
                pe.wait_ge(d.t_ready, i + 1)
                if not first:
                    pe.wait_ge(d.y_ready, i - 1)
                nc.tensor.matmul(psum_y[q][:], ones_r[0:2, :], bias[l][:], start=True, stop=False)
                pairs = [(agg_t, w_a)] if l == 0 else [(x_t, w_s), (agg_t, w_a)]
                for n, (a, w) in enumerate(pairs):
                    for k in range(KT):
                        last = nc.tensor.matmul(psum_y[q][:], a[:, q, k, :], w[:, k, :], start=False,
                                                stop=n == len(pairs) - 1 and k == KT - 1)
                last.then_inc(d.projected, 1)

            def dense_steps(l):
                def step(i, q, first, ahead):
                    if ahead:
                        transposes(l, i + 1, 1 - q, False)
                    project(l, i, q, first)

                transposes(l, 0, 0, True)
                block_steps(pe, step)

            dense_steps(0)

            def sum_group(g, q):
                for c in range(GROUP):
                    nc.tensor.matmul(psum_sum[q][:], sel[:, q, c, :].bitcast(F32), gathered[:, g * GROUP + c, :],
                                     start=c == 0, stop=c == GROUP - 1)
                for c in range(GROUP):
                    last = nc.tensor.matmul(psum_deg[q][:, 0:2], sel[:, q, c, :], ones_r[:, 0:2],
                                            start=c == 0, stop=c == GROUP - 1)
                last.then_inc(summed, 1)

            with pe.If(wide == 0):
                def sum_round(r, first, last):
                    for g in range(RING):
                        G = r * RING + g
                        pe.wait_ge(sel_ready, G + 1)
                        if not (first and g < SEL):
                            pe.wait_ge(added, G - SEL + 1)
                        for c in range(GROUP):
                            pe.wait_ge(rows_in[g * GROUP + c], 16 * (r + 1))
                        sum_group(g, g % SEL)

                rounds(pe, sum_round)
            with pe.Else():
                with pe.Fori(0, GROUPS) as G:
                    with pe.Fori(0, BLOCKS) as b:
                        for c in range(GROUP):
                            pe.wait_ge(rows_in[c], 16 * (G + 1))
                        pe.wait_ge(sel_ready, G * BLOCKS + b + 1)
                        sum_group(0, 0)
            pe.wait_ge(wn_in, 16)
            dense_steps(1)


_ORDER = ["x", "src_t", "dst_t", "w_t", "src_n", "dst_n", "w0", "b0", "w_self", "w_neigh", "b1"]


def kernel(x, src, dst, edge_weight, L0_gnn_weight, L0_gnn_bias, L1_gnn_W_self, L1_gnn_W_neigh, L1_gnn_b):
    import numpy as np
    import concourse.bacc as bacc
    from concourse.bass_utils import run_bass_kernel_spmd

    x = np.asarray(x)
    n, D = x.shape
    E = np.asarray(src).shape[0]
    per_round = RING * GROUP * CHUNK
    total = -(-E // per_round) * per_round

    def padded(a, fill):
        a = np.asarray(a)
        return np.concatenate([a, np.full(total - E, fill, a.dtype)])

    src, dst, w = padded(src, 0), padded(dst, -1), padded(edge_weight, 0)
    blocks = -(-n // P) // 2 * 2 + 1
    arrays = {
        "x": np.concatenate([x, np.zeros((blocks * P - n, D), x.dtype)]),
        "src_t": src.reshape(-1, P).T, "dst_t": dst.reshape(-1, P).T, "w_t": w.reshape(-1, P).T,
        "src_n": src.reshape(-1, GROUP * CHUNK), "dst_n": dst.reshape(-1, GROUP * CHUNK),
        "w0": L0_gnn_weight, "b0": L0_gnn_bias,
        "w_self": np.asarray(L1_gnn_W_self).T, "w_neigh": np.asarray(L1_gnn_W_neigh).T, "b1": L1_gnn_b,
    }
    arrays = {k: np.ascontiguousarray(v) for k, v in arrays.items()}
    nc = bacc.Bacc("TRN2", target_bir_lowering=False, num_devices=1)
    aps = [nc.dram_tensor(f"in_{k}", arrays[k].shape, mybir.dt.from_np(arrays[k].dtype), kind="ExternalInput").ap()
           for k in _ORDER]
    out = nc.dram_tensor("out_0", (blocks * P, D), F32, kind="ExternalOutput").ap()
    gnn_two_layers(nc, *aps, out)
    r = run_bass_kernel_spmd(nc, [{f"in_{k}": arrays[k] for k in _ORDER}], core_ids=[0])
    return np.asarray(r.results[0]["out_0"])[:n]
```

```python
from contextlib import ExitStack

import concourse.bass as bass
from concourse import mybir

F32 = mybir.dt.float32
F32R = mybir.dt.float32r
BF16 = mybir.dt.bfloat16
I32 = mybir.dt.int32
U32 = mybir.dt.uint32
I16 = mybir.dt.int16
ALU = mybir.AluOpType
ACT = mybir.ActivationFunctionType
AX = mybir.AxisListType

P = 128
CHUNK = 128
GROUP = 4
RING = 4
SEL = 2
MSG = 2 * GROUP
ACCS = GROUP
SPLIT = 1
LEAD = 2
EPS = 1e-5
NO_ROW = 1000.0
FAR = 8192.0


def gnn_two_layers(nc, x, src_t, dst_t, w_t, src_n, dst_n, w0, b0, w_self, w_neigh, b1, out):
    rows, D = x.shape
    BLOCKS = rows // P
    CHUNKS = src_t.shape[1]
    GROUPS = CHUNKS // GROUP
    ROUNDS = GROUPS // RING
    HALF = GROUPS // 2
    KT = D // P
    GE = GROUP * CHUNK
    assert BLOCKS % 2 == 1 and BLOCKS >= 5 and GROUPS % RING == 0
    assert rows < 2 ** 15
    assert ROUNDS == BLOCKS

    x1_dram = nc.dram_tensor("x1_dram", [rows, D], F32).ap()
    own_dram = nc.dram_tensor("own_dram", [rows, D], F32).ap()
    acc_tensors = [nc.dram_tensor(f"acc{k}", [rows + P, D], F32).ap() for k in range(ACCS)]
    base_dram = nc.dram_tensor("base_dram", [GROUPS], I32).ap()
    src_dram = nc.dram_tensor("src_dram", [GROUPS, GE], I16).ap()
    wide_dram = nc.dram_tensor("wide_dram", [GROUPS], I32).ap()

    ctx = ExitStack()
    with ctx:
        def sb(name, shape, dt=F32):
            return ctx.enter_context(nc.sbuf_tensor(name, shape, dt))

        def ps(name):
            return ctx.enter_context(nc.psum_tensor(name, [P, 512], F32))

        def sem(name):
            return ctx.enter_context(nc.semaphore(name))

        def lender(flat):
            taken = [0]

            def lend(*shape, parts=P):
                n = 1
                for k in shape:
                    n *= k
                a = flat[0:parts, taken[0]:taken[0] + n]
                taken[0] += n
                assert taken[0] <= flat.shape[1]
                if len(shape) == 2:
                    a = a.rearrange("p (a b) -> p a b", a=shape[0])
                if len(shape) == 3:
                    a = a.rearrange("p (a b c) -> p a b c", a=shape[0], b=shape[1])
                return a

            return lend

        agg = sb("agg", [P, BLOCKS + 1, D])
        deg = sb("deg", [P, BLOCKS + 1])
        gathered = sb("gathered", [P, RING * GROUP, D])
        sel = sb("sel", [P, SEL, GROUP, P], F32R)
        sel_b = sb("sel_b", [P, SEL, GROUP, P], BF16)
        high = sb("high", [P, SEL, SPLIT, D], F32R)
        low = sb("low", [P, SEL, SPLIT, D], F32R)
        idx_all = sb("idx_all", [P, CHUNKS], I32)
        idx_now = [sb(f"idx_now{g}", [P, GROUP], I32) for g in range(RING)]
        to_now = [sb(f"to_now{g}", [P, GROUP], I32) for g in range(RING)]
        dst_f = sb("dst_f", [P, CHUNKS])
        row_f = sb("row_f", [P, CHUNKS])
        in_lo = sb("in_lo", [P, GROUPS])
        in_hi = sb("in_hi", [P, GROUPS])
        blk_i = sb("blk_i", [1, GROUPS], I32)
        from_i = sb("from_i", [1, GROUPS], I32)
        any_f = sb("any_f", [1, 1])
        any_wide = sb("any_wide", [1, 1], I32)
        g_max = sb("g_max", [HALF, 2])
        g_min = sb("g_min", [HALF, 2])
        g_base = sb("g_base", [HALF, 2], I32)
        g_wide_f = sb("g_wide_f", [HALF, 2])
        g_wide = sb("g_wide", [HALF, 2], I32)
        col_f = sb("col_f", [P, P])
        par_i = sb("par_i", [P, 1], I32)
        par_f = sb("par_f", [P, 1])
        ident = sb("ident", [P, P])
        tri = sb("tri", [P, P])
        ones = sb("ones", [P, P])
        ones_r = sb("ones_r", [P, P], F32R)
        ones_b = sb("ones_b", [P, 2], BF16)
        eps = sb("eps", [P, 1])
        w_a = sb("w_a", [P, KT, D])
        w_s = sb("w_s", [P, KT, D])
        bias = [sb(f"bias{l}", [2, D], F32R) for l in range(2)]
        part = sb("part", [2, 2])
        far_dst = sb("far_dst", [P, GROUP])
        staged = sb("staged", [P, 2, D])
        xin = sb("xin", [P, 2, D])
        agg_t = sb("agg_t", [P, 2, KT, P])
        x_t = sb("x_t", [P, 2, KT, P])
        y = sb("y", [P, 2, D])
        xo = sb("xo", [P, 2, D])
        stats = sb("stats", [P, 2, 6])
        mv = sb("mv", [P, 2, 2])
        std = sb("std", [P, 2, 1])
        rstd = sb("rstd", [P, 2, 1])
        shift = sb("shift", [P, 2, 1])
        rdeg = sb("rdeg", [P, BLOCKS + 1])

        own_in = x_t[:].rearrange("p q k n -> p q (k n)")

        lend = lender(gathered[:].rearrange("p a d -> p (a d)"))
        dn_i = lend(2, GE, parts=HALF).bitcast(I32)
        dn_f = lend(2, GE, parts=HALF)
        dn_pad = lend(2, GE, parts=HALF)
        dst_i = lend(CHUNKS).bitcast(I32)
        row_i = lend(CHUNKS).bitcast(I32)
        pad_f = lend(CHUNKS)
        zeros = lend(D)
        base_i = lend(GROUPS).bitcast(I32)
        base_f = lend(GROUPS)
        brow_i = lend(GROUPS).bitcast(I32)
        brow_f = lend(GROUPS)
        wide_row = lend(GROUPS, parts=1).bitcast(I32)
        wide_f = lend(GROUPS, parts=1)
        col_i = lend(P).bitcast(I32)

        lend = lender(agg[:].rearrange("p a d -> p (a d)"))
        accs = lend(2, ACCS * D)
        pair_sum = lend(D)
        FREED = 2 * ACCS + 1
        msg = lend(MSG, D)
        same = lend(SEL, GROUP, P)
        src_all = lend(RING, GE // 2).bitcast(I16)
        window = lend(RING, D)
        near = lend(SEL, GROUP, P)
        mix = lend(SEL, GE)
        dst_near = lend(CHUNKS)
        scratch = lend(GROUP, P)
        src_f = lend(CHUNKS)
        spare_f = lend(CHUNKS)
        gat_all = lend(CHUNKS).bitcast(I32)
        wgt = lend(CHUNKS)
        earlier = lend(SEL, GROUP)
        to_f = lend(SEL, GROUP)
        spare_row = lend(1)
        sn_i = lend(2, GE, parts=HALF).bitcast(I32)
        sn_short = lend(2, GE // 2, parts=HALF).bitcast(I16)
        bias_in = lend(2, D, parts=2)
        bias_hi = lend(2, D, parts=2).bitcast(F32R)
        bias_lo = lend(2, D, parts=2)

        banks = [ps(f"bank{k}") for k in range(8)]
        psum_msg = banks[0:GROUP]
        psum_mix = banks[GROUP:GROUP + SEL]
        psum_sum = banks[0:SEL]
        psum_deg = banks[SEL:2 * SEL]
        psum_t, psum_xt = banks[4:6]
        psum_y = banks[6:8]

        dstn_in = sem("dstn_in")
        srcn_in = sem("srcn_in")
        edges_in = sem("edges_in")
        short_out = sem("short_out")
        acc_zero = sem("acc_zero")
        base_out = sem("base_out")
        base_in = sem("base_in")
        w_in = sem("w_in")
        wn_in = sem("wn_in")
        iotas = sem("iotas")
        prep = sem("prep")
        zeros_ready = sem("zeros_ready")
        short_ready = sem("short_ready")
        groups_known = sem("groups_known")
        flag_ready = sem("flag_ready")
        waited = sem("waited")
        agg_zero = sem("agg_zero")
        layer_summed = sem("layer_summed")

        idx0_ready = sem("idx0_ready")
        rows0_in = [sem(f"rows0_in{k}") for k in range(RING * GROUP)]
        src_all_in = [sem(f"src_all_in{g}") for g in range(RING)]
        window_in = [sem(f"window_in{g}") for g in range(RING)]
        mix_summed = sem("mix_summed")
        mix_ready = sem("mix_ready")
        same_ready = sem("same_ready")
        counted = sem("counted")
        aimed = sem("aimed")
        to_ready = sem("to_ready")
        msg_summed = sem("msg_summed")
        msg_ready = sem("msg_ready")
        msg_added = [sem(f"msg_added{m}") for m in range(MSG)]
        idx_ready = sem("idx_ready")
        rows_in = [sem(f"rows_in{k}") for k in range(RING * GROUP)]
        sel_ready = sem("sel_ready")
        high_ready = sem("high_ready")
        low_ready = sem("low_ready")
        counts_ready = sem("counts_ready")
        summed = sem("summed")
        added = sem("added")

        own_x_in = sem("own_x_in")
        own_transposed = sem("own_transposed")
        own_t_ready = sem("own_t_ready")
        own_projected = sem("own_projected")
        own_ready = sem("own_ready")
        own_stored = sem("own_stored")

        class Dense:
            def __init__(self, l):
                self.xin_ready = [sem(f"xin_ready{l}{q}") for q in range(2)]
                self.staged = sem(f"staged{l}")
                self.transposed = sem(f"transposed{l}")
                self.t_ready = sem(f"t_ready{l}")
                self.projected = sem(f"projected{l}")
                self.y_ready = sem(f"y_ready{l}")
                self.stat = sem(f"stat{l}")
                self.var_ready = sem(f"var_ready{l}")
                self.std_ready = sem(f"std_ready{l}")
                self.rstd_ready = sem(f"rstd_ready{l}")
                self.norm_ready = sem(f"norm_ready{l}")
                self.normed = sem(f"normed{l}")
                self.stored = [sem(f"stored{l}{q}") for q in range(2)]

        dense = [Dense(l) for l in range(2)]
        accs_in = [sem(f"accs_in{q}") for q in range(2)]
        acc_sum = sem("acc_sum")
        deg1_ready = sem("deg1_ready")
        rdeg_ready = sem("rdeg_ready")
        own_added = sem("own_added")

        def row_of(t, b):
            return t[:, b, :] if isinstance(b, int) else t[:, bass.ds(b, 1), :].rearrange("p o d -> p (o d)")

        def general(eng):
            return eng.value_load(any_wide[0:1, 0:1], min_val=0, max_val=1)

        def alone(eng):
            eng.sem_inc(waited, 1)

        def rounds(eng, one_round):
            one_round(0, True, False)
            with eng.Fori(1, ROUNDS - 1) as r:
                one_round(r, False, False)
            one_round(ROUNDS - 1, False, True)

        def block_steps(eng, step):
            step(0, 0, True, 2)
            step(1, 1, True, 2)
            step(2, 0, False, 2)
            with eng.Fori(3, BLOCKS - 3, 2) as i:
                step(i, 1, False, 2)
                step(i + 1, 0, False, 2)
            step(BLOCKS - 2, 1, False, 1)
            step(BLOCKS - 1, 0, False, 0)

        def half(i, q):
            return (i - q) // 2

        def all_stored(eng, d):
            eng.wait_ge(d.stored[0], 16 * (BLOCKS // 2 + 1))
            eng.wait_ge(d.stored[1], 16 * (BLOCKS // 2))

        block = ctx.enter_context(nc.Block())

        @block.sync
        def _(sp):
            sp.dma_start(dn_i, dst_n.rearrange("(p t) e -> p t e", p=HALF)).then_inc(dstn_in, 16)
            sp.dma_start(sn_i, src_n.rearrange("(p t) e -> p t e", p=HALF)).then_inc(srcn_in, 16)
            for t, a in ((idx_all[:], src_t), (dst_i, dst_t), (wgt, w_t)):
                sp.dma_start(t, a).then_inc(edges_in, 16)
            for l, a in enumerate((b0, b1)):
                sp.dma_start(bias_in[:, l, :], a.rearrange("(o n) -> o n", o=1).broadcast_to([2, D])).then_inc(edges_in, 16)
            sp.wait_ge(zeros_ready, 1)

            def zero(k):
                sp.dma_start(acc_tensors[k].rearrange("(b p) d -> p b d", p=P),
                             zeros.rearrange("p (o d) -> p o d", o=1).broadcast_to([P, BLOCKS + 1, D])).then_inc(acc_zero, 16)

            zero(0)
            sp.wait_ge(short_ready, 1)
            sp.dma_start(src_dram.rearrange("(p t) e -> p t e", p=HALF), sn_short).then_inc(short_out, 16)
            sp.wait_ge(groups_known, 1)
            sp.dma_start(base_dram.rearrange("(p t) -> p t", p=HALF), g_base[:]).then_inc(base_out, 16)
            sp.dma_start(wide_dram.rearrange("(p t) -> p t", p=HALF), g_wide[:]).then_inc(base_out, 16)
            zero(1)
            sp.wait_ge(base_out, 32)
            sp.dma_start(base_i, base_dram.rearrange("(o g) -> o g", o=1).broadcast_to([P, GROUPS])).then_inc(base_in, 16)
            sp.dma_start(wide_row, wide_dram.rearrange("(o g) -> o g", o=1)).then_inc(base_in, 16)

            sp.wait_ge(flag_ready, 1)
            wide = general(sp)
            sp.wait_ge(short_out, 16)

            def source_rounds(windows):
                def source_round(r, first, last):
                    for g in range(RING):
                        G = r * RING + g
                        if not first:
                            sp.wait_ge(to_ready, G - RING + 1)
                        sp.dma_start(src_all[:, g, :], src_dram[bass.ds(G, 1), :].broadcast_to([P, GE])).then_inc(src_all_in[g], 16)
                        if windows:
                            v = sp.value_load(from_i[0:1, bass.ds(G, 1)], min_val=0, max_val=rows - P)
                            if not first:
                                sp.wait_ge(msg_summed, (G - RING + 1) * GROUP)
                            sp.dma_start(window[:, g, :], x[bass.ds(v, P), :]).then_inc(window_in[g], 16)

                source_round(0, True, False)
                for k in range(2, ACCS):
                    zero(k)
                for t, a in ((w_a, w0), (w_s, w_self)):
                    sp.dma_start(t[:], a.rearrange("(k p) n -> p k n", p=P)).then_inc(w_in, 16)
                with sp.Fori(1, ROUNDS) as r:
                    source_round(r, False, False)

            with sp.If(wide == 0):
                source_rounds(True)
            with sp.Else():
                source_rounds(False)

            for m in range(MSG):
                sp.wait_ge(msg_added[m], 16 * (CHUNKS // MSG))
            d0 = dense[0]

            def load_accs(i, q):
                for k in range(ACCS):
                    sp.dma_start(accs[:, q, k * D:(k + 1) * D], acc_tensors[k][bass.ds(i * P, P), :]).then_inc(accs_in[q], 16)

            def step0(i, q, first, ahead):
                if ahead == 2:
                    sp.wait_ge(acc_sum, i + 1)
                    load_accs(i + 2, q)

            for i in range(2):
                load_accs(i, i)
            block_steps(sp, step0)
            sp.wait_ge(d0.projected, BLOCKS)
            sp.dma_start(w_a[:], w_neigh.rearrange("(k p) n -> p k n", p=P)).then_inc(wn_in, 16)
            all_stored(sp, d0)

            def own_load(r, first, last):
                if not first:
                    sp.wait_ge(own_transposed, r)
                sp.dma_start(xin[:, 0, :], x1_dram[bass.ds(r * P, P), :]).then_inc(own_x_in, 16)

            rounds(sp, own_load)
            sp.wait_ge(own_stored, 16 * BLOCKS)
            d1 = dense[1]

            def load1(i, q):
                sp.dma_start(own_in[:, q, :], own_dram[bass.ds(i * P, P), :]).then_inc(d1.xin_ready[q], 16)
                sp.dma_start(xin[:, q, :], x1_dram[bass.ds(i * P, P), :]).then_inc(d1.xin_ready[q], 16)

            def step1(i, q, first, ahead):
                if ahead == 2:
                    sp.wait_ge(d1.y_ready, i + 1)
                    load1(i + 2, q)

            load1(0, 0)
            load1(1, 1)
            block_steps(sp, step1)
            all_stored(sp, d1)

        @block.gpsimd
        def _(pool):
            nc.gpsimd.iota(col_i, pattern=[[1, P]], base=0, channel_multiplier=0).then_inc(iotas, 1)
            nc.gpsimd.iota(par_i[:], pattern=[[0, 1]], base=0, channel_multiplier=1).then_inc(iotas, 1)

            def gather(table, sems, g, c):
                nc.gpsimd.indirect_dma_start(
                    gathered[:, g * GROUP + c, :], None, table,
                    bass.IndirectOffsetOnAxis(idx_now[g][:, c:c + 1].bitcast(U32), axis=0),
                ).then_inc(sems[g * GROUP + c], 16)

            pool.wait_ge(flag_ready, 1)
            wide = general(pool)

            def gather0(r, g, first):
                G = r * RING + g
                if not first:
                    pool.wait_ge(msg_summed, (G - RING + 1) * GROUP)
                pool.wait_ge(idx0_ready, G + 1)
                alone(pool)
                for c in range(GROUP):
                    gather(x, rows0_in, g, c)

            def add0(r, g, first):
                G = r * RING + g
                pool.wait_ge(to_ready, G + 1)
                for c in range(GROUP):
                    m, before = g % 2 * GROUP + c, (g % 2 * GROUP + c + MSG - ACCS) % MSG
                    turn = r * (RING // 2) + g // 2
                    pool.wait_ge(msg_ready, G * GROUP + c + 1)
                    if m >= ACCS:
                        pool.wait_ge(msg_added[before], 16 * (turn + 1))
                    elif not (first and g < 2):
                        pool.wait_ge(msg_added[before], 16 * turn)
                    alone(pool)
                    nc.gpsimd.indirect_dma_start(
                        acc_tensors[c],
                        bass.IndirectOffsetOnAxis(to_now[g][:, c:c + 1].bitcast(U32), axis=0),
                        msg[:, m, :], None, compute_op=ALU.add,
                    ).then_inc(msg_added[m], 16)

            pool.wait_ge(acc_zero, 16 * ACCS)
            with pool.If(wide == 0):
                def round0(r, first, last):
                    for g in range(RING):
                        add0(r, g, first)

                rounds(pool, round0)
            with pool.Else():
                for g in range(LEAD):
                    gather0(0, g, True)

                def round0(r, first, last):
                    for g in range(RING):
                        if g + LEAD < RING:
                            gather0(r, g + LEAD, first)
                        elif not last:
                            gather0(r + 1, g + LEAD - RING, False)
                        add0(r, g, first)

                rounds(pool, round0)
            for m in range(MSG):
                pool.wait_ge(msg_added[m], 16 * (CHUNKS // MSG))
            nc.gpsimd.memset(agg[:, FREED:BLOCKS + 1, :], 0.0).then_inc(agg_zero, 1)
            all_stored(pool, dense[0])
            with pool.If(wide == 0):
                def gather_round(r, first, last):
                    for g in range(RING):
                        if not first:
                            pool.wait_ge(summed, (r - 1) * RING + g + 1)
                        pool.wait_ge(idx_ready, r * RING + g + 1)
                        alone(pool)
                        for c in range(GROUP):
                            gather(x1_dram, rows_in, g, c)

                rounds(pool, gather_round)
            with pool.Else():
                def gather_group(G, first):
                    if not first:
                        pool.wait_ge(summed, G * BLOCKS)
                    pool.wait_ge(idx_ready, G + 1)
                    alone(pool)
                    for c in range(GROUP):
                        gather(x1_dram, rows_in, 0, c)

                gather_group(0, True)
                with pool.Fori(1, GROUPS) as G:
                    gather_group(G, False)

        @block.scalar
        def _(act):
            act.wait_ge(flag_ready, 1)
            wide = general(act)

            def place0(r, g, first):
                G = r * RING + g
                if not first:
                    act.wait_ge(msg_summed, (G - RING + 1) * GROUP)
                nc.scalar.copy(idx_now[g][:], gat_all[:, bass.ds(G * GROUP, GROUP)]).then_inc(idx0_ready, 1)

            def evict0(r, g, first):
                G = r * RING + g
                for c in range(GROUP):
                    m = g % 2 * GROUP + c
                    act.wait_ge(msg_summed, G * GROUP + c + 1)
                    if not (first and g < 2):
                        act.wait_ge(msg_added[m], 16 * (r * (RING // 2) + g // 2))
                    nc.scalar.activation(msg[:, m, :], psum_msg[c][:], ACT.Copy).then_inc(msg_ready, 1)

            def mix_out(r, g, first):
                G = r * RING + g
                act.wait_ge(mix_summed, G + 1)
                if not (first and g < SEL):
                    act.wait_ge(msg_summed, (G - SEL + 1) * GROUP)
                nc.scalar.activation(mix[:, g % SEL, :], psum_mix[g % SEL][:], ACT.Copy).then_inc(mix_ready, 1)

            with act.If(wide == 0):
                def round0(r, first, last):
                    for g in range(RING):
                        if g + 1 < RING:
                            mix_out(r, g + 1, first)
                        elif not last:
                            mix_out(r + 1, 0, False)
                        evict0(r, g, first)

                mix_out(0, 0, True)
                rounds(act, round0)
            with act.Else():
                for g in range(RING - 1):
                    place0(0, g, True)

                def round0(r, first, last):
                    for g in range(RING):
                        if g == 0:
                            place0(r, RING - 1, first)
                        elif not last:
                            place0(r + 1, g - 1, False)
                        evict0(r, g, first)

                rounds(act, round0)

            def transposes_out(l, i, q, first):
                d = dense[l]
                act.wait_ge(d.transposed, i + 1)
                if not first:
                    act.wait_ge(d.projected, i - 1)
                nc.scalar.activation(agg_t[:, q, :, :], psum_t[:].rearrange("p (k n) -> p k n", k=KT), ACT.Copy).then_inc(d.t_ready, 1)

            def norm(l, i, q, first):
                d = dense[l]
                act.wait_ge(d.var_ready, i + 1)
                nc.scalar.activation(std[:, q, :], mv[:, q, 1:2], ACT.Sqrt, bias=eps[:]).then_inc(d.std_ready, 1)
                act.wait_ge(d.norm_ready, i + 1)
                if not first:
                    act.wait_ge(d.stored[q], 16 * half(i, q))
                nc.scalar.activation(xo[:, q, :], y[:, q, :], ACT.Identity, bias=shift[:, q, :],
                                     scale=rstd[:, q, :]).then_inc(d.normed, 1)

            def store(l, i, q):
                act.wait_ge(dense[l].normed, i + 1)
                act.dma_start((x1_dram, out)[l][bass.ds(i * P, P), :], xo[:, q, :]).then_inc(dense[l].stored[q], 16)

            def norm_before(l, i, q):
                if isinstance(i, int) and i == 0:
                    return
                norm(l, i - 1, 1 - q, isinstance(i, int) and i <= 2)
                store(l, i - 1, 1 - q)

            def step0(i, q, first, ahead):
                if ahead:
                    transposes_out(0, i + 1, 1 - q, first and q == 0)
                norm_before(0, i, q)
                if ahead and not (first and q == 0):
                    load_x(i + 1, 1 - q)

            def load_x(i, q):
                act.dma_start(xin[:, q, :], x[bass.ds(i * P, P), :]).then_inc(dense[0].xin_ready[q], 16)

            for i in range(2):
                load_x(i, i)
            transposes_out(0, 0, 0, True)
            block_steps(act, step0)
            norm_before(0, BLOCKS, 1)
            all_stored(act, dense[0])

            def own_turn(r, first):
                act.wait_ge(own_transposed, r + 1)
                if not first:
                    act.wait_ge(own_projected, r)
                nc.scalar.activation(x_t[:, 0, :, :], psum_xt[:].rearrange("p (k n) -> p k n", k=KT), ACT.Copy).then_inc(own_t_ready, 1)

            def own_out(r, first):
                act.wait_ge(own_projected, r + 1)
                if not first:
                    act.wait_ge(own_stored, 16 * r)
                nc.scalar.activation(xo[:, 0, :], psum_y[0][:], ACT.Copy).then_inc(own_ready, 1)
                act.wait_ge(own_ready, r + 1)
                act.dma_start(own_dram[bass.ds(r * P, P), :], xo[:, 0, :]).then_inc(own_stored, 16)

            with act.If(wide == 0):
                def place(r, g, first):
                    if not first:
                        act.wait_ge(summed, (r - 1) * RING + g + 1)
                    nc.scalar.copy(idx_now[g][:], idx_all[:, bass.ds((r * RING + g) * GROUP, GROUP)]).then_inc(idx_ready, 1)

                def cut(r, g, first):
                    if not (first and g < SEL):
                        act.wait_ge(summed, r * RING + g - SEL + 1)
                    for c in range(SPLIT):
                        act.wait_ge(rows_in[g * GROUP + c], 16 * (r + 1))
                        nc.scalar.copy(high[:, g % SEL, c, :], gathered[:, g * GROUP + c, :]).then_inc(high_ready, 1)

                def place_round(r, first, last):
                    for g in range(RING):
                        G = r * RING + g
                        if g < 2:
                            place(r, g + 2, first)
                        elif not last:
                            place(r + 1, g - 2, False)
                        act.wait_ge(sel_ready, G + 1)
                        if not (first and g < SEL):
                            act.wait_ge(summed, G - SEL + 1)
                        nc.scalar.copy(sel_b[:, g % SEL, :, :], sel[:, g % SEL, :, :].bitcast(F32)).then_inc(counts_ready, 1)
                        if g + 1 < RING:
                            cut(r, g + 1, first)
                        elif not last:
                            cut(r + 1, 0, False)
                        if g == 0 and not first:
                            own_out(r - 1, False)
                        if g == 1:
                            own_turn(r, first)

                place(0, 0, True)
                place(0, 1, True)
                cut(0, 0, True)
                rounds(act, place_round)
                own_out(ROUNDS - 1, False)
            with act.Else():
                def own_round(r, first, last):
                    own_turn(r, first)
                    own_out(r, first)

                rounds(act, own_round)

                def place_group(G, first):
                    if not first:
                        act.wait_ge(summed, G * BLOCKS)
                    nc.scalar.copy(idx_now[0][:], idx_all[:, bass.ds(G * GROUP, GROUP)]).then_inc(idx_ready, 1)

                place_group(0, True)
                with act.Fori(1, GROUPS) as G:
                    place_group(G, False)
            d1 = dense[1]
            act.wait_ge(layer_summed, 1)
            act.wait_ge(own_stored, 16 * BLOCKS)

            def stage(i, q, first):
                if not first:
                    act.wait_ge(d1.transposed, i - 1)
                nc.scalar.activation(staged[:, q, :], row_of(agg, i), ACT.Copy, scale=rdeg[:, bass.ds(i, 1)]).then_inc(d1.staged, 1)

            def step1(i, q, first, ahead):
                if ahead:
                    transposes_out(1, i + 1, 1 - q, first and q == 0)
                if ahead == 2:
                    stage(i + 2, q, False)
                norm_before(1, i, q)

            act.wait_ge(rdeg_ready, 1)
            stage(0, 0, True)
            stage(1, 1, True)
            transposes_out(1, 0, 0, True)
            block_steps(act, step1)
            norm_before(1, BLOCKS, 1)

        @block.vector
        def _(dve):
            steps = [0]

            def then(ins):
                steps[0] += 1
                ins.then_inc(prep, 1)
                dve.wait_ge(prep, steps[0])

            nc.vector.memset(zeros, 0.0).then_inc(zeros_ready, 1)
            dve.wait_ge(dstn_in, 16)
            then(nc.vector.tensor_copy(dn_f, dn_i))
            nc.vector.tensor_reduce(g_max[:], dn_f, AX.X, ALU.max)
            then(nc.vector.tensor_scalar(dn_pad, dn_f, 0.0, FAR, ALU.is_lt, ALU.mult))
            then(nc.vector.tensor_tensor(dn_pad, dn_pad, dn_f, ALU.add))
            then(nc.vector.tensor_reduce(g_min[:], dn_pad, AX.X, ALU.min))
            then(nc.vector.tensor_scalar(g_min[:], g_min[:], float(rows - P), None, ALU.min))
            nc.vector.tensor_copy(g_base[:], g_min[:])
            then(nc.vector.tensor_tensor(g_wide_f[:], g_max[:], g_min[:], ALU.subtract))
            nc.vector.tensor_scalar(g_wide[:], g_wide_f[:], float(P), None, ALU.is_ge).then_inc(groups_known, 1)
            dve.wait_ge(srcn_in, 16)
            nc.vector.tensor_copy(sn_short, sn_i).then_inc(short_ready, 1)
            nc.vector.memset(ones[:], 1.0)
            nc.vector.memset(eps[:], EPS)
            then(nc.vector.memset(deg[:], 0.0))
            nc.vector.tensor_copy(ones_r[:], ones[:])
            nc.vector.tensor_copy(ones_b[:], ones[:, 0:2])
            dve.wait_ge(iotas, 2)
            nc.vector.tensor_copy(col_f[:], col_i)
            then(nc.vector.tensor_copy(par_f[:], par_i[:]))
            nc.vector.tensor_scalar(ident[:], col_f[:], par_f[:], None, ALU.is_equal)
            nc.vector.tensor_scalar(tri[:], col_f[:], par_f[:], None, ALU.is_lt)
            nc.vector.tensor_scalar(spare_row, par_f[:], float(rows), None, ALU.add)
            dve.wait_ge(edges_in, 80)
            nc.vector.tensor_copy(dst_f[:], dst_i)
            nc.vector.tensor_copy(src_f, idx_all[:])
            then(nc.vector.tensor_scalar(row_i, dst_i, P - 1, None, ALU.bitwise_and))
            nc.vector.tensor_scalar(spare_f, src_f, -1.0, spare_row, ALU.mult, ALU.add)
            nc.vector.tensor_scalar(gat_all, dst_f[:], 0.0, None, ALU.max)
            nc.vector.tensor_copy(row_f[:], row_i)
            then(nc.vector.tensor_scalar(pad_f, dst_f[:], 0.0, NO_ROW, ALU.is_lt, ALU.mult))
            then(nc.vector.tensor_tensor(row_f[:], row_f[:], pad_f, ALU.add))
            nc.vector.tensor_scalar(part[:, 0:1], par_f[0:2, :], 0.0, None, ALU.is_equal)
            nc.vector.tensor_scalar(part[:, 1:2], par_f[0:2, :], 1.0, None, ALU.is_equal)
            then(nc.vector.tensor_copy(bias_hi, bias_in))
            then(nc.vector.tensor_tensor(bias_lo, bias_in, bias_hi.bitcast(F32), ALU.subtract))
            then(nc.vector.tensor_scalar(bias_lo, bias_lo, part[:, 1:2], None, ALU.mult))
            for l in range(2):
                nc.vector.scalar_tensor_tensor(bias[l][:], bias_hi[:, l, :].bitcast(F32), part[:, 0:1], bias_lo[:, l, :], ALU.mult, ALU.add)
            dve.wait_ge(base_in, 32)
            nc.vector.tensor_copy(from_i[:], base_i[0:1, :])
            then(nc.vector.tensor_copy(base_f, base_i))
            nc.vector.tensor_tensor(dst_near.rearrange("p (g c) -> p g c", c=GROUP), dst_f[:].rearrange("p (g c) -> p g c", c=GROUP),
                                    base_f.rearrange("p (g o) -> p g o", o=1).broadcast_to([P, GROUPS, GROUP]), ALU.subtract)
            nc.vector.tensor_scalar(blk_i[:], base_i[0:1, :], 7, None, ALU.logical_shift_right)
            then(nc.vector.tensor_scalar(brow_i, base_i, P - 1, None, ALU.bitwise_and))
            then(nc.vector.tensor_copy(brow_f, brow_i))
            then(nc.vector.tensor_scalar(in_lo[:], brow_f, par_f[:], None, ALU.is_le))
            nc.vector.tensor_scalar(in_hi[:], in_lo[:], -1.0, 1.0, ALU.mult, ALU.add)
            then(nc.vector.tensor_copy(wide_f, wide_row))
            then(nc.vector.tensor_reduce(any_f[:], wide_f, AX.X, ALU.max))
            nc.vector.tensor_copy(any_wide[:], any_f[:]).then_inc(flag_ready, 1)
            dve.wait_ge(flag_ready, 1)
            wide = general(dve)

            def match_rounds(windows):
                def match_round(r, first, last):
                    for g in range(RING):
                        G, q = r * RING + g, g % SEL
                        turn = r * (RING // 2) + g // 2
                        if not (first and g < SEL):
                            if windows:
                                dve.wait_ge(mix_summed, G - SEL + 1)
                            else:
                                dve.wait_ge(msg_summed, (G - SEL + 1) * GROUP)
                        if windows:
                            nc.vector.tensor_tensor(near[:, q, :, :], col_f[:].rearrange("p (o m) -> p o m", o=1).broadcast_to([P, GROUP, P]),
                                                    dst_near[:, bass.ds(G * GROUP, GROUP)].rearrange("p (c o) -> p c o", o=1).broadcast_to([P, GROUP, P]),
                                                    ALU.is_equal)
                        dve.wait_ge(src_all_in[g], 16 * (r + 1))
                        for c in range(GROUP):
                            col = G * GROUP + c
                            last_op = nc.vector.tensor_scalar(same[:, q, c, :], src_all[:, g, c * P:(c + 1) * P],
                                                              src_f[:, bass.ds(col, 1)], wgt[:, bass.ds(col, 1)],
                                                              ALU.is_equal, ALU.mult)
                        last_op.then_inc(same_ready, 1)
                        if not (first and g == 0):
                            dve.wait_ge(counted, G)
                        for c in range(GROUP):
                            last_op = nc.vector.scalar_tensor_tensor(scratch[:, c, :], src_all[:, g, c * P:(c + 1) * P],
                                                                     src_f[:, bass.ds(G * GROUP + c, 1)], tri[:],
                                                                     ALU.is_equal, ALU.mult, accum_out=earlier[:, q, c:c + 1])
                        last_op.then_inc(counted, 1)
                        dve.wait_ge(counted, G + 1)
                        nc.vector.scalar_tensor_tensor(to_f[:, q, :], earlier[:, q, :], 0.5, spare_f[:, bass.ds(G * GROUP, GROUP)],
                                                       ALU.is_ge, ALU.mult).then_inc(aimed, 1)
                        dve.wait_ge(aimed, G + 1)
                        if not first:
                            for c in range(GROUP):
                                dve.wait_ge(msg_added[g % 2 * GROUP + c], 16 * (turn - 1))
                        nc.vector.tensor_tensor(to_now[g][:], to_f[:, q, :], src_f[:, bass.ds(G * GROUP, GROUP)],
                                                ALU.add).then_inc(to_ready, 1)

                rounds(dve, match_round)

            with dve.If(wide == 0):
                match_rounds(True)
            with dve.Else():
                match_rounds(False)

            def sum_accs(i, q, first):
                dve.wait_ge(accs_in[q], 16 * ACCS * (half(i, q) + 1))
                if not first:
                    dve.wait_ge(dense[0].transposed, i - 1)
                nc.vector.tensor_tensor(staged[:, q, :], accs[:, q, 0:D], accs[:, q, D:2 * D], ALU.add)
                if not (first and q == 0):
                    dve.wait_ge(dense[0].staged, i)
                nc.vector.tensor_tensor(pair_sum, accs[:, q, 2 * D:3 * D], accs[:, q, 3 * D:4 * D], ALU.add).then_inc(acc_sum, 1)
                dve.wait_ge(acc_sum, i + 1)
                nc.vector.tensor_tensor(staged[:, q, :], staged[:, q, :], pair_sum, ALU.add).then_inc(dense[0].staged, 1)

            def moments(l, i, q, first):
                d = dense[l]
                dve.wait_ge(d.projected, i + 1)
                dve.wait_ge(d.xin_ready[q], (16, 32)[l] * (half(i, q) + 1))
                if not first:
                    dve.wait_ge(d.normed, i - 1)
                if l == 0:
                    nc.vector.tensor_tensor(y[:, q, :], psum_y[q][:], xin[:, q, :], ALU.add).then_inc(d.y_ready, 1)
                else:
                    nc.vector.tensor_tensor(y[:, q, :], psum_y[q][:], own_in[:, q, :], ALU.add).then_inc(own_added, 1)
                    dve.wait_ge(own_added, i + 1)
                    nc.vector.scalar_tensor_tensor(y[:, q, :], y[:, q, :], 0.0, xin[:, q, :], ALU.max, ALU.add).then_inc(d.y_ready, 1)
                dve.wait_ge(d.y_ready, i + 1)
                nc.vector.bn_stats(stats[:, q, :], y[:, q, :]).then_inc(d.stat, 1)
                dve.wait_ge(d.stat, i + 1)
                alone(dve)
                nc.vector.bn_aggr(mv[:, q, :], stats[:, q, :]).then_inc(d.var_ready, 1)

            def scales(l, i, q):
                d = dense[l]
                dve.wait_ge(d.std_ready, i + 1)
                nc.vector.reciprocal(rstd[:, q, :], std[:, q, :]).then_inc(d.rstd_ready, 1)
                dve.wait_ge(d.rstd_ready, i + 1)
                nc.vector.scalar_tensor_tensor(shift[:, q, :], mv[:, q, 0:1], -1.0, rstd[:, q, :], ALU.mult, ALU.mult
                                               ).then_inc(d.norm_ready, 1)

            def dense_steps(l):
                def step(i, q, first, ahead):
                    if l == 0 and ahead == 2:
                        sum_accs(i + 2, q, False)
                    moments(l, i, q, first)
                    scales(l, i, q)

                if l == 0:
                    sum_accs(0, 0, True)
                    sum_accs(1, 1, True)
                block_steps(dve, step)

            dense_steps(0)
            dve.wait_ge(dense[0].normed, BLOCKS)
            nc.vector.memset(agg[:, 0:FREED, :], 0.0).then_inc(agg_zero, 1)
            dve.wait_ge(agg_zero, 2)
            with dve.If(wide == 0):
                def select(r, g, first):
                    q, G = g % SEL, r * RING + g
                    if not (first and g < SEL):
                        dve.wait_ge(summed, G - SEL + 1)
                    nc.vector.tensor_tensor(sel[:, q, :, :], col_f[:].rearrange("p (o m) -> p o m", o=1).broadcast_to([P, GROUP, P]),
                                            row_f[:, bass.ds(G * GROUP, GROUP)].rearrange("p (c o) -> p c o", o=1).broadcast_to([P, GROUP, P]),
                                            ALU.is_equal).then_inc(sel_ready, 1)

                def leave(r, g, first):
                    G = r * RING + g
                    for c in range(SPLIT):
                        dve.wait_ge(high_ready, G * SPLIT + c + 1)
                        nc.vector.tensor_tensor(low[:, g % SEL, c, :], gathered[:, g * GROUP + c, :], high[:, g % SEL, c, :].bitcast(F32),
                                                ALU.subtract).then_inc(low_ready, 1)

                def add(G, g, first):
                    q = g % SEL
                    b = dve.value_load(blk_i[0:1, bass.ds(G, 1)], min_val=0, max_val=BLOCKS - 1)
                    dve.wait_ge(summed, G + 1)
                    if not first:
                        dve.wait_ge(added, G)
                    for at, mask in ((b, in_lo), (b + 1, in_hi)):
                        m = mask[:, bass.ds(G, 1)]
                        nc.vector.scalar_tensor_tensor(deg[:, bass.ds(at, 1)], psum_deg[q][:, 0:1], m,
                                                       deg[:, bass.ds(at, 1)], ALU.mult, ALU.add)
                        last = nc.vector.scalar_tensor_tensor(row_of(agg, at), psum_sum[q][:], m, row_of(agg, at),
                                                              ALU.mult, ALU.add)
                    last.then_inc(added, 1)

                def sum_round(r, first, last):
                    for g in range(RING):
                        select(r, g, first)
                        leave(r, g, first)
                        if not (first and g == 0):
                            add(r * RING + g - 1, g - 1, first and g == 1)

                rounds(dve, sum_round)
                add(GROUPS - 1, RING - 1, False)
            with dve.Else():
                nc.vector.memset(far_dst[:], 0.0).then_inc(added, 1)
                with dve.Fori(0, GROUPS) as G:
                    dve.wait_ge(added, G * (BLOCKS + 1) + 1)
                    nc.vector.tensor_copy(far_dst[:], dst_f[:, bass.ds(G * GROUP, GROUP)]).then_inc(added, 1)
                    with dve.Fori(0, BLOCKS) as b:
                        dve.wait_ge(added, G * (BLOCKS + 1) + b + 2)
                        for c in range(GROUP):
                            nc.vector.tensor_scalar(sel_b[:, 0, c, :], col_f[:], far_dst[:, c:c + 1], None, ALU.is_equal)
                            last = nc.vector.tensor_scalar(sel[:, 0, c, :], col_f[:], far_dst[:, c:c + 1], None, ALU.is_equal)
                        last.then_inc(sel_ready, 1)
                        dve.wait_ge(summed, G * BLOCKS + b + 1)
                        nc.vector.tensor_tensor(row_of(agg, b), psum_sum[0][:], row_of(agg, b), ALU.add)
                        nc.vector.tensor_tensor(deg[:, bass.ds(b, 1)], psum_deg[0][:, 0:1], deg[:, bass.ds(b, 1)], ALU.add)
                        nc.vector.tensor_scalar(far_dst[:], far_dst[:], float(P), None, ALU.subtract).then_inc(added, 1)
            dve.drain().then_inc(layer_summed, 1)
            dve.wait_ge(layer_summed, 1)
            nc.vector.tensor_scalar(deg[:], deg[:], 1.0, None, ALU.max).then_inc(deg1_ready, 1)
            dve.wait_ge(deg1_ready, 1)
            nc.vector.reciprocal(rdeg[:], deg[:]).then_inc(rdeg_ready, 1)
            dense_steps(1)

        @block.tensor
        def _(pe):
            pe.wait_ge(flag_ready, 1)
            wide = general(pe)

            def message(r, g, c, first, weights, table):
                if not (first and g == 0):
                    pe.wait_ge(msg_ready, (r * RING + g - 1) * GROUP + c + 1)
                nc.tensor.matmul(psum_msg[c][:], weights, table, start=True, stop=True).then_inc(msg_summed, 1)

            with pe.If(wide == 0):
                def mix_group(r, g, first):
                    G, q = r * RING + g, g % SEL
                    pe.wait_ge(same_ready, G + 1)
                    if not (first and g < SEL):
                        pe.wait_ge(mix_ready, G - SEL + 1)
                    for c in range(GROUP):
                        last = nc.tensor.matmul(psum_mix[q][:, c * P:(c + 1) * P], near[:, q, c, :], same[:, q, c, :],
                                                start=True, stop=True)
                    last.then_inc(mix_summed, 1)

                def message_round(r, first, last):
                    for g in range(RING):
                        G, q = r * RING + g, g % SEL
                        if g + 1 < RING:
                            mix_group(r, g + 1, first)
                        elif not last:
                            mix_group(r + 1, 0, False)
                        pe.wait_ge(mix_ready, G + 1)
                        pe.wait_ge(window_in[g], 16 * (r + 1))
                        for c in range(GROUP):
                            message(r, g, c, first, mix[:, q, c * P:(c + 1) * P], window[:, g, :])

                mix_group(0, 0, True)
                rounds(pe, message_round)
            with pe.Else():
                def message_round(r, first, last):
                    for g in range(RING):
                        pe.wait_ge(same_ready, r * RING + g + 1)
                        for c in range(GROUP):
                            pe.wait_ge(rows0_in[g * GROUP + c], 16 * (r + 1))
                            message(r, g, c, first, same[:, g % SEL, c, :], gathered[:, g * GROUP + c, :])

                rounds(pe, message_round)

            def transposes(l, i, q, first):
                d = dense[l]
                pe.wait_ge(d.staged, i + 1)
                if not first:
                    pe.wait_ge(d.t_ready, i)
                for k in range(KT):
                    last = nc.tensor.transpose(psum_t[:, k * P:(k + 1) * P], staged[:, q, k * P:(k + 1) * P], ident[:])
                last.then_inc(d.transposed, 1)

            def project(l, i, q, first):
                d = dense[l]
                pe.wait_ge(d.t_ready, i + 1)
                if not first:
                    pe.wait_ge(d.y_ready, i - 1)
                if l == 0:
                    nc.tensor.matmul(psum_y[q][:], ones_r[0:2, :], bias[0][:], start=True, stop=False)
                for k in range(KT):
                    last = nc.tensor.matmul(psum_y[q][:], agg_t[:, q, k, :], w_a[:, k, :], start=l == 1 and k == 0,
                                            stop=k == KT - 1)
                last.then_inc(d.projected, 1)

            def dense_steps(l):
                def step(i, q, first, ahead):
                    if ahead:
                        transposes(l, i + 1, 1 - q, False)
                    project(l, i, q, first)

                transposes(l, 0, 0, True)
                block_steps(pe, step)

            pe.wait_ge(w_in, 32)
            dense_steps(0)

            def own_transposes(r, first):
                pe.wait_ge(own_x_in, 16 * (r + 1))
                if not first:
                    pe.wait_ge(own_t_ready, r)
                for k in range(KT):
                    last = nc.tensor.transpose(psum_xt[:, k * P:(k + 1) * P], xin[:, 0, k * P:(k + 1) * P], ident[:])
                last.then_inc(own_transposed, 1)

            def own_products(r, first, part):
                if part == 0:
                    pe.wait_ge(own_t_ready, r + 1)
                    if not first:
                        pe.wait_ge(own_ready, r)
                    nc.tensor.matmul(psum_y[0][:], ones_r[0:2, :], bias[1][:], start=True, stop=False)
                for k in range(part * KT // 2, (part + 1) * KT // 2):
                    last = nc.tensor.matmul(psum_y[0][:], x_t[:, 0, k, :], w_s[:, k, :], start=False, stop=k == KT - 1)
                if part == 1:
                    last.then_inc(own_projected, 1)

            def sum_chunks(g, q, chunks):
                for c in chunks:
                    nc.tensor.matmul(psum_sum[q][:], sel[:, q, c, :].bitcast(F32), gathered[:, g * GROUP + c, :],
                                     start=c == 0, stop=c == GROUP - 1)

            def sum_split(G, q, c):
                pe.wait_ge(low_ready, G * SPLIT + c + 1)
                for k, part in enumerate((high, low)):
                    nc.tensor.matmul(psum_sum[q][:], sel[:, q, c, :], part[:, q, c, :], start=c + k == 0, stop=False)

            def count(q):
                for c in range(GROUP):
                    last = nc.tensor.matmul(psum_deg[q][:, 0:2], sel_b[:, q, c, :], ones_b[:],
                                            start=c == 0, stop=c == GROUP - 1)
                last.then_inc(summed, 1)

            with pe.If(wide == 0):
                def sum_round(r, first, last):
                    for g in range(RING):
                        G = r * RING + g
                        if g == 0:
                            own_transposes(r, first)
                        if g >= 2:
                            own_products(r, first, g - 2)
                        pe.wait_ge(counts_ready, G + 1)
                        if not (first and g < SEL):
                            pe.wait_ge(added, G - SEL + 1)
                        for c in range(SPLIT):
                            sum_split(G, g % SEL, c)
                        for c in range(SPLIT, GROUP):
                            pe.wait_ge(rows_in[g * GROUP + c], 16 * (r + 1))
                            sum_chunks(g, g % SEL, [c])
                        count(g % SEL)

                rounds(pe, sum_round)
            with pe.Else():
                def own_round(r, first, last):
                    own_transposes(r, first)
                    own_products(r, first, 0)
                    own_products(r, first, 1)

                rounds(pe, own_round)
                with pe.Fori(0, GROUPS) as G:
                    with pe.Fori(0, BLOCKS) as b:
                        for c in range(GROUP):
                            pe.wait_ge(rows_in[c], 16 * (G + 1))
                        pe.wait_ge(sel_ready, G * BLOCKS + b + 1)
                        sum_chunks(0, 0, range(GROUP))
                        count(0)
            pe.wait_ge(wn_in, 16)
            dense_steps(1)


_ORDER = ["x", "src_t", "dst_t", "w_t", "src_n", "dst_n", "w0", "b0", "w_self", "w_neigh", "b1"]


def kernel(x, src, dst, edge_weight, L0_gnn_weight, L0_gnn_bias, L1_gnn_W_self, L1_gnn_W_neigh, L1_gnn_b):
    import numpy as np
    import concourse.bacc as bacc
    from concourse.bass_utils import run_bass_kernel_spmd

    x = np.asarray(x)
    n, D = x.shape
    E = np.asarray(src).shape[0]
    per_round = RING * GROUP * CHUNK
    total = -(-E // per_round) * per_round

    def padded(a, fill):
        a = np.asarray(a)
        return np.concatenate([a, np.full(total - E, fill, a.dtype)])

    src, dst, w = padded(src, 0), padded(dst, -1), padded(edge_weight, 0)
    blocks = -(-n // P) // 2 * 2 + 1
    arrays = {
        "x": np.concatenate([x, np.zeros((blocks * P - n, D), x.dtype)]),
        "src_t": src.reshape(-1, P).T, "dst_t": dst.reshape(-1, P).T, "w_t": w.reshape(-1, P).T,
        "src_n": src.reshape(-1, GROUP * CHUNK), "dst_n": dst.reshape(-1, GROUP * CHUNK),
        "w0": L0_gnn_weight, "b0": L0_gnn_bias,
        "w_self": np.asarray(L1_gnn_W_self).T, "w_neigh": np.asarray(L1_gnn_W_neigh).T, "b1": L1_gnn_b,
    }
    arrays = {k: np.ascontiguousarray(v) for k, v in arrays.items()}
    nc = bacc.Bacc("TRN2", target_bir_lowering=False, num_devices=1)
    aps = [nc.dram_tensor(f"in_{k}", arrays[k].shape, mybir.dt.from_np(arrays[k].dtype), kind="ExternalInput").ap()
           for k in _ORDER]
    out = nc.dram_tensor("out_0", (blocks * P, D), F32, kind="ExternalOutput").ap()
    gnn_two_layers(nc, *aps, out)
    r = run_bass_kernel_spmd(nc, [{f"in_{k}": arrays[k] for k in _ORDER}], core_ids=[0])
    return np.asarray(r.results[0]["out_0"])[:n]
```
